# Optimizing a Trainium2 kernel written in Bass

```python
import numpy as np
import jax
import jax.numpy as jnp

def _softmax(x, axis=-1):
    return jax.nn.softmax(x, axis=axis)

def _gelu(x):
    return jax.nn.gelu(x, approximate=True)

def _silu(x):
    return jax.nn.silu(x)

def _sigmoid(x):
    return jax.nn.sigmoid(x)

def _layernorm(x, axis=-1, eps=1e-05):
    m = jnp.mean(x, axis=axis, keepdims=True)
    v = jnp.var(x, axis=axis, keepdims=True)
    return (x - m) / jnp.sqrt(v + eps)

def _scatter_add(tgt, idx, src, axis=0):
    return tgt.at[idx].add(src)

def _segment_sum(src, seg, n):
    return jax.ops.segment_sum(src, seg, n)
kernel_name = 'mk_prb_d1_jaxref_r8_2254c7'

def setup_inputs(seed: int=0):
    np.random.seed(seed)
    _w = jnp.asarray

    def _L0_attn_setup():
        import jax, jax.numpy as jnp
        import numpy as np
        B, S, H = (1, 256, 512)
        NH = 32
        QK_NOPE, QK_ROPE, V_DIM = (128, 64, 128)
        Q_LORA, KV_LORA = (192, 64)
        EPS = 1e-06

        def _rms_norm(x, w):
            return x * jax.lax.rsqrt(jnp.mean(x * x, axis=-1, keepdims=True) + EPS) * w

        def _rope_cos_sin(seqlen, dim):
            freqs = 1.0 / 10000.0 ** (jnp.arange(0, dim, 2, dtype=jnp.float32) / dim)
            t = jnp.arange(seqlen, dtype=jnp.float32)
            ang = jnp.outer(t, freqs)
            return (jnp.cos(ang), jnp.sin(ang))

        def _apply_rope(x, cos, sin):
            x1 = x[..., 0::2]
            x2 = x[..., 1::2]
            r1 = x1 * cos - x2 * sin
            r2 = x1 * sin + x2 * cos
            return jnp.stack([r1, r2], axis=-1).reshape(x.shape)
        key = jax.random.key(seed)
        ks = jax.random.split(key, 7)
        s = 0.02
        return {'x': jax.random.normal(ks[0], (B, S, H), jnp.float32), 'wq_a': jax.random.normal(ks[1], (Q_LORA, H), jnp.float32) * s, 'q_norm_w': jnp.ones((Q_LORA,), jnp.float32), 'wq_b': jax.random.normal(ks[2], (NH * (QK_NOPE + QK_ROPE), Q_LORA), jnp.float32) * s, 'wkv_a': jax.random.normal(ks[3], (KV_LORA + QK_ROPE, H), jnp.float32) * s, 'kv_norm_w': jnp.ones((KV_LORA,), jnp.float32), 'wkv_b': jax.random.normal(ks[4], (NH * (QK_NOPE + V_DIM), KV_LORA), jnp.float32) * s, 'wo': jax.random.normal(ks[5], (H, NH * V_DIM), jnp.float32) * s}
    _L0_attn_in = _L0_attn_setup()

    def _L0_ffn_setup():
        import jax, jax.numpy as jnp
        import numpy as np
        M = 512
        K = 512

        def _make_2to4_mask(key, shape):
            scores = jax.random.normal(key, shape)
            g = scores.reshape(shape[0], shape[1] // 4, 4)
            rank = jnp.argsort(jnp.argsort(-jnp.abs(g), axis=-1), axis=-1)
            return (rank < 2).reshape(shape).astype(jnp.float32)
        key = jax.random.key(seed)
        k_x, k_w12, k_b12, k_w3, k_b3, k_m = jax.random.split(key, 6)
        x = jax.random.normal(k_x, (4, 256, K), dtype=jnp.float32)
        w12_dense = jax.random.normal(k_w12, (2 * M, K), dtype=jnp.float32) * (1.0 / np.sqrt(K))
        mask12 = _make_2to4_mask(k_m, (2 * M, K))
        w12 = w12_dense * mask12
        b12 = jax.random.normal(k_b12, (2 * M,), dtype=jnp.float32) * 0.01
        w3 = jax.random.normal(k_w3, (M, M), dtype=jnp.float32) * (1.0 / np.sqrt(M))
        b3 = jax.random.normal(k_b3, (M,), dtype=jnp.float32) * 0.01
        return {'x': x, 'w12': w12, 'b12': b12, 'w3': w3, 'b3': b3}
    _L0_ffn_in = _L0_ffn_setup()
    _d = {'L0_attn_x': _L0_attn_in['x'], 'L0_attn_wq_a': _L0_attn_in['wq_a'], 'L0_attn_q_norm_w': _L0_attn_in['q_norm_w'], 'L0_attn_wq_b': _L0_attn_in['wq_b'], 'L0_attn_wkv_a': _L0_attn_in['wkv_a'], 'L0_attn_kv_norm_w': _L0_attn_in['kv_norm_w'], 'L0_attn_wkv_b': _L0_attn_in['wkv_b'], 'L0_attn_wo': _L0_attn_in['wo'], 'L0_ffn_w12': _L0_ffn_in['w12'], 'L0_ffn_b12': _L0_ffn_in['b12'], 'L0_ffn_w3': _L0_ffn_in['w3'], 'L0_ffn_b3': _L0_ffn_in['b3']}
    _x0 = _d['L0_attn_x']
    _d['L0_attn_x'] = jax.random.normal(jax.random.fold_in(jax.random.key(seed), 1), (2, 1024, 512), dtype=_x0.dtype)
    del _x0
    return _d

def reference(L0_attn_x, L0_attn_wq_a, L0_attn_q_norm_w, L0_attn_wq_b, L0_attn_wkv_a, L0_attn_kv_norm_w, L0_attn_wkv_b, L0_attn_wo, L0_ffn_w12, L0_ffn_b12, L0_ffn_w3, L0_ffn_b3):

    def _L0_attn_ref(x, wq_a, q_norm_w, wq_b, wkv_a, kv_norm_w, wkv_b, wo):
        import jax, jax.numpy as jnp
        import numpy as np
        B, S, H = (1, 256, 512)
        NH = 32
        QK_NOPE, QK_ROPE, V_DIM = (128, 64, 128)
        Q_LORA, KV_LORA = (192, 64)
        EPS = 1e-06

        def _rms_norm(x, w):
            return x * jax.lax.rsqrt(jnp.mean(x * x, axis=-1, keepdims=True) + EPS) * w

        def _rope_cos_sin(seqlen, dim):
            freqs = 1.0 / 10000.0 ** (jnp.arange(0, dim, 2, dtype=jnp.float32) / dim)
            t = jnp.arange(seqlen, dtype=jnp.float32)
            ang = jnp.outer(t, freqs)
            return (jnp.cos(ang), jnp.sin(ang))

        def _apply_rope(x, cos, sin):
            x1 = x[..., 0::2]
            x2 = x[..., 1::2]
            r1 = x1 * cos - x2 * sin
            r2 = x1 * sin + x2 * cos
            return jnp.stack([r1, r2], axis=-1).reshape(x.shape)
        b, s, _ = x.shape
        cos, sin = _rope_cos_sin(s, QK_ROPE)
        q = _rms_norm(x @ wq_a.T, q_norm_w) @ wq_b.T
        q = q.reshape(b, s, NH, QK_NOPE + QK_ROPE)
        q_nope, q_pe = (q[..., :QK_NOPE], q[..., QK_NOPE:])
        q_pe = _apply_rope(q_pe, cos[None, :, None, :], sin[None, :, None, :])
        kv = x @ wkv_a.T
        kv_c, k_pe = (kv[..., :KV_LORA], kv[..., KV_LORA:])
        k_pe = _apply_rope(k_pe, cos[None, :, :], sin[None, :, :])
        kv_up = _rms_norm(kv_c, kv_norm_w) @ wkv_b.T
        kv_up = kv_up.reshape(b, s, NH, QK_NOPE + V_DIM)
        k_nope, v = (kv_up[..., :QK_NOPE], kv_up[..., QK_NOPE:])
        scale = 1.0 / jnp.sqrt(jnp.float32(QK_NOPE + QK_ROPE))
        scores = (jnp.einsum('bshd,bthd->bhst', q_nope, k_nope) + jnp.einsum('bshd,btd->bhst', q_pe, k_pe)) * scale
        causal = jnp.tril(jnp.ones((s, s), bool))
        scores = jnp.where(causal[None, None], scores, jnp.finfo(scores.dtype).min)
        probs = jax.nn.softmax(scores, axis=-1)
        out = jnp.einsum('bhst,bthd->bshd', probs, v).reshape(b, s, NH * V_DIM)
        return out @ wo.T

    def _L0_ffn_ref(x, w12, b12, w3, b3):
        import jax, jax.numpy as jnp
        import numpy as np
        M = 512
        K = 512

        def _make_2to4_mask(key, shape):
            scores = jax.random.normal(key, shape)
            g = scores.reshape(shape[0], shape[1] // 4, 4)
            rank = jnp.argsort(jnp.argsort(-jnp.abs(g), axis=-1), axis=-1)
            return (rank < 2).reshape(shape).astype(jnp.float32)
        x12 = jnp.einsum('bsk,mk->bsm', x, w12) + b12
        x1, x2 = jnp.split(x12, 2, axis=-1)
        x4 = jax.nn.silu(x1) * x2
        return jnp.einsum('bsm,nm->bsn', x4, w3) + b3
    x = L0_attn_x
    xn = _layernorm(x, axis=-1)
    x = x + _L0_attn_ref(xn, L0_attn_wq_a, L0_attn_q_norm_w, L0_attn_wq_b, L0_attn_wkv_a, L0_attn_kv_norm_w, L0_attn_wkv_b, L0_attn_wo) + _L0_ffn_ref(xn, L0_ffn_w12, L0_ffn_b12, L0_ffn_w3, L0_ffn_b3)
    return x

_drawn_inputs = setup_inputs


def setup_inputs(seed=0):
    import zlib

    import numpy as np

    out = dict(_drawn_inputs(seed))
    spreads = {'L0_attn_q_norm_w': (1.0, 0.6), 'L0_attn_kv_norm_w': (1.0, 0.6)}
    factors = {'L0_attn_wq_a': 8.0,
     'L0_attn_wq_b': 8.0,
     'L0_attn_wkv_a': 3.233,
     'L0_attn_wkv_b': 3.196,
     'L0_attn_wo': 3.264,
     'L0_ffn_b12': 8.0,
     'L0_ffn_b3': 6.118}
    for name, (base, spread) in spreads.items():
        noise = np.random.default_rng([zlib.crc32(name.encode()), seed]).standard_normal(out[name].shape)
        drawn = base * np.exp(spread * noise) if base else spread * noise
        out[name] = jnp.asarray(drawn.astype(out[name].dtype))
    for name, factor in factors.items():
        out[name] = (out[name] * factor).astype(out[name].dtype)
    return out
```

```python
import numpy as np
from contextlib import ExitStack

import concourse.bass as bass
from concourse import mybir
from concourse.alu_op_type import AluOpType as ALU

ACT = mybir.ActivationFunctionType
AX = mybir.AxisListType
F32 = mybir.dt.float32
F32R = mybir.dt.float32r
F16 = mybir.dt.float16
BF16 = mybir.dt.bfloat16

P = 128
B, S, H = 2, 1024, 512
NH, NOPE, ROPE, VD = 32, 128, 64, 128
QL, KVL = 192, 64
FF = 512
TOK = B * S
NT = TOK // P
ST = S // P
KH = H // P
LAT = QL + KVL + ROPE
PAIRS = NH // 2
SCALE = 1.0 / float(np.sqrt(np.float32(NOPE + ROPE)))
LN_EPS, RMS_EPS = 1e-5, 1e-6
WQ = 2 * 3 * P
ds = bass.ds


def absorb_weights(nc, io, scr):
    with ExitStack() as ctx:
        sb = lambda n, s, d: ctx.enter_context(nc.sbuf_tensor(n + "_sb", s, d))
        ps = lambda n, s, d: ctx.enter_context(nc.psum_tensor(n, s, d))
        sem = lambda n: ctx.enter_context(nc.semaphore(n))
        wqn = sb("wqn", [P, 2, 2, QL], F32)
        wk = sb("wk", [P, 2, 2, KVL], F32)
        wv = sb("wv", [P, 2, 2, KVL], F32)
        wo = sb("wo", [P, 2, 2, H], F32)
        kvw2 = sb("kvw2", [P, 1], F32)
        wf = sb("wf", [P, 2, WQ], F32)
        wh = sb("wh", [P, 2, WQ], F32R)
        wl = sb("wl", [P, 2, WQ], F32R)
        of = sb("of", [P, 2, H], F32)
        oh = sb("oh", [P, 2, H], F32R)
        ol = sb("ol", [P, 2, H], F32R)
        credit = sb("credit", [P, 4], F32)
        pq = [ps(f"pq{i}", [P, 512], F32) for i in range(2)]
        po = [ps(f"po{i}", [P, 512], F32) for i in range(2)]
        zeroed = sem("zeroed")
        loaded = [sem("w_loaded0"), sem("w_loaded1")]
        const_in = sem("kvw_in")
        q_mm, o_mm = sem("absorbed_q"), sem("absorbed_o")
        q_full, q_hi, q_lo = sem("wq_full"), sem("wq_hi"), sem("wq_lo")
        o_full, o_hi, o_lo = sem("wo_full"), sem("wo_hi"), sem("wo_lo")
        stored = [sem("w_stored0"), sem("w_stored1")]
        NLOAD, NSTORE = 8, 4
        block = ctx.enter_context(nc.Block())

        def load(sp, pair, j):
            for dst, src in (
                (wqn[:, j], io["wqn"][:, ds(2 * pair, 2), :]), (wk[:, j], io["wk"][:, ds(2 * pair, 2), :]),
                (wv[:, j], io["wv"][:, ds(2 * pair, 2), :]), (wo[:, j], io["wo"][:, ds(2 * pair, 2), :]),
                (wf[:, j, P // 2:P // 2 + P], io["wqp0"][:, ds(pair, 1), 0:P]),
                (wf[:, j, 2 * P:3 * P], io["wqp0"][:, ds(pair, 1), P:2 * P]),
                (wf[0:64, j, 3 * P + 64:3 * P + 64 + P], io["wqp1"][:, ds(pair, 1), 0:P]),
                (wf[0:64, j, 5 * P:6 * P], io["wqp1"][:, ds(pair, 1), P:2 * P]),
            ):
                sp.dma_start(dst, src).then_inc(loaded[j], 16)

        @block.sync
        def _(sp):
            sp.dma_start(kvw2[:], io["kvw2"]).then_inc(const_in, 16)
            sp.wait_ge(zeroed, 2)
            load(sp, 0, 0)
            load(sp, 1, 1)
            with sp.Fori(0, PAIRS // 2) as it:
                after = [sp.snap((2 * it + j + 2) % PAIRS) for j in range(2)]
                for j in range(2):
                    sp.wait_ge(q_lo, 2 * it + j + 1)
                    sp.wait_ge(o_lo, 2 * it + j + 1)
                    pair = 2 * it + j
                    for src, dst in ((wh, "wq_hi"), (wl, "wq_lo"), (oh, "wo_hi"), (ol, "wo_lo")):
                        sp.dma_start(scr[dst][:, ds(pair, 1), :], src[:, j:j + 1, :].bitcast(F32)).then_inc(stored[j], 16)
                    sp.wait_ge(stored[j], 16 * NSTORE * (it + 1))
                    load(sp, after[j], j)
            for j in range(2):
                sp.wait_ge(stored[j], 16 * NSTORE * (PAIRS // 2))
                sp.wait_ge(loaded[j], 16 * NLOAD * (PAIRS // 2 + 1))

        @block.tensor
        def _(pe):
            with pe.Fori(0, PAIRS // 2) as it:
                for j in range(2):
                    pe.wait_ge(loaded[j], 16 * NLOAD * (it + 1))
                    pe.wait_ge(q_full, 2 * it + j + 1)
                    for h in range(2):
                        nc.tensor.matmul(pq[j][:, h * KVL:(h + 1) * KVL], wqn[:, j, h, 0:P], wk[:, j, h, :],
                                         start=True, stop=True)
                    for h in range(2):
                        mm = nc.tensor.matmul(pq[j][0:QL - P, P + h * KVL:P + (h + 1) * KVL], wqn[:, j, h, P:QL],
                                              wk[:, j, h, :], start=True, stop=True)
                    mm.then_inc(q_mm, 1)
                    pe.wait_ge(o_full, 2 * it + j + 1)
                    for h in range(2):
                        mm = nc.tensor.matmul(po[j][h * KVL:(h + 1) * KVL, :], wv[:, j, h, :], wo[:, j, h, :],
                                              start=True, stop=True)
                    mm.then_inc(o_mm, 1)

        @block.scalar
        def _(act):
            act.wait_ge(const_in, 16)
            for j in range(2):
                nc.scalar.activation(credit[:, 2 * j:2 * j + 1], kvw2[:], ACT.Copy).then_inc(q_full, 1)
                nc.scalar.activation(credit[:, 2 * j + 1:2 * j + 2], kvw2[:], ACT.Copy).then_inc(o_full, 1)
            with act.Fori(0, PAIRS // 2) as it:
                for j in range(2):
                    n = 2 * it + j
                    act.wait_ge(q_mm, n + 1)
                    at = wf[:, j, 0:3 * P].rearrange("p (g c) -> p g c", c=KVL)[:, 0:4:3, :]
                    nc.scalar.activation(at, pq[j][:, 0:P].rearrange("p (g c) -> p g c", c=KVL), ACT.Copy)
                    at = wf[0:64, j, 3 * P:6 * P].rearrange("p (g c) -> p g c", c=KVL)[:, 0:4:3, :]
                    nc.scalar.activation(at, pq[j][0:64, P:2 * P].rearrange("p (g c) -> p g c", c=KVL),
                                         ACT.Copy).then_inc(q_full, 1)
                    act.wait_ge(q_full, n + 3)
                    nc.scalar.activation(wh[:, j, :], wf[:, j, :], ACT.Copy).then_inc(q_hi, 1)
                    act.wait_ge(o_mm, n + 1)
                    nc.scalar.activation(of[:, j, :], po[j][:], ACT.Copy, scale=kvw2[:, 0:1]).then_inc(o_full, 1)
                    act.wait_ge(o_full, n + 3)
                    nc.scalar.activation(oh[:, j, :], of[:, j, :], ACT.Copy).then_inc(o_hi, 1)

        @block.vector
        def _(dve):
            for j in range(2):
                nc.vector.memset(wf[:, j, :], 0.0).then_inc(zeroed, 1)
            with dve.Fori(0, PAIRS // 2) as it:
                for j in range(2):
                    n = 2 * it + j
                    dve.wait_ge(q_hi, n + 1)
                    nc.vector.tensor_tensor(wl[:, j, :], wf[:, j, :], wh[:, j, :].bitcast(F32),
                                            ALU.subtract).then_inc(q_lo, 1)
                    dve.wait_ge(o_hi, n + 1)
                    nc.vector.tensor_tensor(ol[:, j, :], of[:, j, :], oh[:, j, :].bitcast(F32),
                                            ALU.subtract).then_inc(o_lo, 1)



def dense(nc, io, scr, res):
    qk_hi, qk_lo, c16 = res["qk_hi"], res["qk_lo"], res["c16"]
    TC = 4
    NCH = NT // TC
    MT = FF // P
    with ExitStack() as ctx:
        sb = lambda n, s, d: ctx.enter_context(nc.sbuf_tensor(n + "_sb", s, d))
        sem = lambda n: ctx.enter_context(nc.semaphore(n))
        banks = [ctx.enter_context(nc.psum_tensor(f"bank{i}", [P, 512], F32)) for i in range(8)]
        w12h, w12l = sb("w12h", [P, KH, 2 * FF], F32R), sb("w12l", [P, KH, 2 * FF], F32R)
        w3h, w3l = sb("w3h", [P, MT, H], F32R), sb("w3l", [P, MT, H], F32R)
        wlh, wll = sb("wlh", [P, KH, LAT], F32R), sb("wll", [P, KH, LAT], F32R)
        ident = sb("ident", [P, P], F32)
        b12 = sb("b12", [P, 2 * MT], F32)
        nb1 = sb("nb1", [P, MT], F32)
        b3 = sb("b3", [P, H], F32)
        cos, sin = sb("cos_tok", [P, ST, ROPE // 2], F32), sb("sin_tok", [P, ST, ROPE // 2], F32)
        wcol = sb("wcol", [P, 4], F32)
        scl = sb("scl", [P, 4], F32)
        eps = sb("eps", [P, 2], F32)
        x = sb("x", [P, TC, H], F32)
        xn = sb("xn", [P, TC, H], F32)
        stage = xn[:].rearrange("p t c -> p (t c)").rearrange("p (j c) -> p j c", j=2)
        st6, mv = sb("st6", [P, TC, 6], F32), sb("mv", [P, TC, 2], F32)
        fence = sb("fence", [P, 1], F32)
        sd, rsd = sb("sd", [P, TC], F32), sb("rsd", [P, TC], F32)
        xh, xl = sb("xh", [P, KH, TC * P], F32R), sb("xl", [P, KH, TC * P], F32R)
        lat = sb("lat", [P, TC, LAT], F32)
        junk = sb("junk", [P, TC, QL + KVL], BF16)
        ss, rms, rrms = sb("ss", [P, 2, TC], F32), sb("rms", [P, 2, TC], F32), sb("rrms", [P, 2, TC], F32)
        qn = sb("qn", [P, TC, QL], F32)
        kn = sb("kn", [P, TC, KVL + ROPE + KVL], F32)
        rt = sb("rt", [P, 4, TC, ROPE // 2], F32)
        qkf = lat[:].rearrange("p t c -> p (t c)")[:, 0:8 * P].rearrange("p (j k c) -> p j k c", j=2, k=4)
        e1 = sb("e1", [P, 2, 512], F32)
        hf = sb("hf", [P, 2, 512], F32)
        hh, hl = sb("hh", [P, MT, 512], F32R), sb("hl", [P, MT, 512], F32R)

        w_in, w_hi, w_lo = [sem("w_in0"), sem("w_in1")], sem("w_hi"), sem("w_lo")
        c_in, c_set, c_ready = sem("c_in"), sem("c_set"), sem("c_ready")
        x_in, y_init = sem("x_in"), sem("y_init")
        stats, mv_ready, sd_ready, rsd_ready, xn_ready = sem("stats"), sem("mv_ready"), sem("sd_ready"), sem("rsd_ready"), sem("xn_ready")
        xt_mm, xh_ready, xl_ready = sem("xt_mm"), sem("xh_ready"), sem("xl_ready")
        lat_mm, ss_ready, lat_ready, rms_ready, rrms_ready = sem("lat_mm"), sem("ss_ready"), sem("lat_ready"), sem("rms_ready"), sem("rrms_ready")
        qn_ready, cn_ready, c16_hi, rot_mul, rot_ready = sem("qn_ready"), sem("cn_ready"), sem("c16_hi"), sem("rot_mul"), sem("rot_ready")
        kt_mm, qkf_ready, qkh_ready, qkl_ready = sem("kt_mm"), sem("qkf_ready"), sem("qkh_ready"), sem("qkl_ready")
        up_mm, exp_ready, e1_ready, rec_ready, g_ready, hf_ready, hh_ready, hl_ready = (
            sem(n) for n in ("up_mm", "exp_ready", "e1_ready", "rec_ready", "g_ready", "hf_ready", "hh_ready", "hl_ready"))
        down_mm, y_ready, y_out = sem("down_mm"), sem("y_ready"), sem("y_out")
        pieces = [("w12", k, 1, w12h, w12l) for k in range(KH)]
        pieces = [("w_lat", 0, 2, wlh, wll), ("w_lat", 2, 2, wlh, wll)] + pieces
        pieces += [("w3", 0, 2, w3h, w3l), ("w3", 2, 2, w3h, w3l)]
        NP = len(pieces)

        def staged(i):
            name, k, n, hi, lo = pieces[i]
            w = io[name].shape[2]
            return stage[:, i % 2, 0:n * w].rearrange("p (k c) -> p k c", k=n), hi[:, k:k + n, :], lo[:, k:k + n, :]

        block = ctx.enter_context(nc.Block())

        @block.sync
        def _(sp):
            sp.dma_start(x[:], io["x"][:, 0:TC, :]).then_inc(x_in, 16)
            sp.wait_ge(c_set, 1)
            for dst, src in ((ident[:], io["ident"]), (b12[:], io["b12"]), (b3[:], io["b3"].broadcast_to([P, H])),
                             (cos[:], io["cos_tok"]), (sin[:], io["sin_tok"]), (wcol[:, 0:1], io["qnw0"]),
                             (wcol[0:64, 1:2], io["qnw1"]), (wcol[0:64, 2:3], io["kvw"]), (wcol[64:P, 3:4], io["kvw"])):
                sp.dma_start(dst, src).then_inc(c_in, 16)
            for i in range(NP):
                if i >= 2:
                    sp.wait_ge(w_lo, i - 1)
                name, k, n, _, _ = pieces[i]
                sp.dma_start(staged(i)[0], io[name][:, k:k + n, :]).then_inc(w_in[i % 2], 16)
            with sp.Fori(0, NCH - 1) as n:
                for t in range(TC):
                    sp.wait_ge(y_ready, TC * n + t + 1)
                    sp.dma_start(scr["y"][:, ds(TC * n + t, 1), :], x[:, t:t + 1, :]).then_inc(y_out, 16)
                sp.wait_ge(y_out, 16 * TC * (n + 1))
                sp.dma_start(x[:], io["x"][:, ds(TC * n + TC, TC), :]).then_inc(x_in, 16)
            for t in range(TC):
                sp.wait_ge(y_ready, TC * (NCH - 1) + t + 1)
                sp.dma_start(scr["y"][:, TC * (NCH - 1) + t, :], x[:, t, :]).then_inc(y_out, 16)
            sp.wait_ge(y_out, 16 * NT)

        @block.gpsimd
        def _(pool):
            pool.wait_ge(c_in, 16 * 9)
            half = ROPE // 2
            with pool.Fori(0, NCH) as n:
                pool.wait_ge(xn_ready, TC * (n + 1))
                for t in range(TC):
                    op = nc.gpsimd.tensor_tensor(x[:, t, :], x[:, t, :], b3[:], ALU.add)
                op.then_inc(y_init, 1)
                pool.wait_ge(lat_ready, TC * (n + 1))
                c = cos[:, ds(TC * (n % 2), TC), :]
                s = sin[:, ds(TC * (n % 2), TC), :]
                ev, od = lat[:, :, LAT - ROPE:LAT - half], lat[:, :, LAT - half:LAT]
                nc.gpsimd.tensor_tensor(rt[:, 0], ev, c, ALU.mult)
                nc.gpsimd.tensor_tensor(rt[:, 1], od, s, ALU.mult)
                nc.gpsimd.tensor_tensor(rt[:, 2], ev, s, ALU.mult)
                nc.gpsimd.tensor_tensor(rt[:, 3], od, c, ALU.mult).then_inc(rot_mul, 1)
                pool.wait_ge(rot_mul, n + 1)
                nc.gpsimd.tensor_tensor(kn[:, :, KVL:KVL + half], rt[:, 0], rt[:, 1], ALU.subtract)
                nc.gpsimd.tensor_tensor(kn[:, :, KVL + half:KVL + ROPE], rt[:, 2], rt[:, 3],
                                        ALU.add).then_inc(rot_ready, 1)

        @block.scalar
        def _(act):
            def split_weights(i):
                act.wait_ge(w_in[i % 2], 16 * (i // 2 + 1))
                src, hi, _ = staged(i)
                nc.scalar.activation(hi, src, ACT.Copy).then_inc(w_hi, 1)

            def up_exp(n, m):
                act.wait_ge(up_mm, MT * n + m + 1)
                nc.scalar.activation(e1[:, m % 2, :], banks[4 + 2 * (m % 2)][:], ACT.Exp, bias=nb1[:, m:m + 1],
                                     scale=-1.0).then_inc(exp_ready, 1)

            def hidden_hi(n, m):
                act.wait_ge(hf_ready, MT * n + m + 1)
                nc.scalar.activation(hh[:, m, :], hf[:, m % 2, :], ACT.Copy).then_inc(hh_ready, 1)

            for i in range(NP):
                split_weights(i)
            act.wait_ge(c_ready, 3)
            with act.Fori(0, NCH) as n:
                act.wait_ge(mv_ready, TC * (n + 1))
                nc.scalar.activation(sd[:], mv[:, :, 1], ACT.Sqrt, bias=eps[:, 0:1]).then_inc(sd_ready, 1)
                for t in range(TC):
                    act.wait_ge(xt_mm, TC * n + t + 1)
                    nc.scalar.activation(xh[:, :, t * P:(t + 1) * P],
                                         banks[t % 2][:].rearrange("p (k c) -> p k c", k=KH), ACT.Copy).then_inc(xh_ready, 1)
                for t in range(TC):
                    act.wait_ge(lat_mm, TC * n + t + 1)
                    bank = banks[2 + t % 2]
                    nc.scalar.activation(junk[:, t, 0:QL], bank[:, 0:QL], ACT.Square, accum_out=ss[:, 0, t:t + 1])
                    nc.scalar.activation(junk[:, t, QL:QL + KVL], bank[:, QL:QL + KVL], ACT.Square,
                                         accum_out=ss[:, 1, t:t + 1]).then_inc(ss_ready, 1)
                    nc.scalar.activation(lat[:, t, :], bank[:, 0:LAT], ACT.Copy).then_inc(lat_ready, 1)
                act.wait_ge(ss_ready, TC * (n + 1))
                nc.scalar.activation(rms[:, 0, :], ss[:, 0, :], ACT.Sqrt, bias=eps[:, 1:2], scale=1.0 / QL)
                nc.scalar.activation(rms[:, 1, :], ss[:, 1, :], ACT.Sqrt, bias=eps[:, 1:2],
                                     scale=1.0 / KVL).then_inc(rms_ready, 1)
                up_exp(n, 0)
                for m in range(1, MT):
                    up_exp(n, m)
                    hidden_hi(n, m - 1)
                hidden_hi(n, MT - 1)
                for t in range(TC):
                    act.wait_ge(kt_mm, TC * n + t + 1)
                    if t >= 2:
                        act.wait_ge(qkl_ready, TC * n + t - 1)
                    bank = banks[2 + t % 2]
                    for kind in range(4):
                        rows = QL - P if kind == 1 else P
                        op = nc.scalar.activation(qkf[0:rows, t % 2, kind, :], bank[0:rows, kind * P:(kind + 1) * P],
                                                  ACT.Copy, scale=scl[0:rows, kind:kind + 1])
                    op.then_inc(qkf_ready, 1)
                    act.wait_ge(qkf_ready, TC * n + t + 1)
                    nc.scalar.activation(qk_hi[:, :, ds(TC * P * n + t * P, P)], qkf[:, t % 2], ACT.Copy).then_inc(qkh_ready, 1)

        @block.vector
        def _(dve):
            nc.vector.memset(wcol[:], 1.0).then_inc(c_set, 1)
            nc.vector.memset(eps[:, 0:1], LN_EPS)
            nc.vector.memset(eps[:, 1:2], RMS_EPS)
            dve.wait_ge(c_in, 16 * 9)
            nc.vector.tensor_scalar(nb1[:], b12[:, 0:MT], -1.0, None, ALU.mult).then_inc(c_ready, 1)
            nc.vector.tensor_copy(scl[:, 0:2], wcol[:, 0:2]).then_inc(c_ready, 1)
            nc.vector.tensor_scalar(scl[:, 2:4], wcol[:, 2:4], -SCALE, None, ALU.mult).then_inc(c_ready, 1)
            for i in range(NP):
                dve.wait_ge(w_hi, i + 1)
                src, hi, lo = staged(i)
                nc.vector.tensor_tensor(lo, src, hi.bitcast(F32), ALU.subtract).then_inc(w_lo, 1)

            def hidden_lo(n, m):
                dve.wait_ge(hh_ready, MT * n + m + 1)
                nc.vector.tensor_tensor(hl[:, m, :], hf[:, m % 2, :], hh[:, m, :].bitcast(F32),
                                        ALU.subtract).then_inc(hl_ready, 1)

            with dve.Fori(0, NCH) as n:
                dve.wait_ge(x_in, 16 * (n + 1))
                for t in range(TC):
                    nc.vector.bn_stats(st6[:, t, :], x[:, t, :]).then_inc(stats, 1)
                dve.wait_ge(stats, TC * (n + 1))
                nc.vector.memset(fence[:], 0.0)
                for t in range(TC):
                    nc.vector.bn_aggr(mv[:, t, :], st6[:, t, :]).then_inc(mv_ready, 1)
                dve.wait_ge(sd_ready, n + 1)
                nc.vector.reciprocal(rsd[:], sd[:]).then_inc(rsd_ready, 1)
                dve.wait_ge(rsd_ready, n + 1)
                for t in range(TC):
                    nc.vector.tensor_scalar(xn[:, t, :], x[:, t, :], mv[:, t, 0:1], rsd[:, t:t + 1],
                                            ALU.subtract, ALU.mult).then_inc(xn_ready, 1)
                for t in range(TC):
                    dve.wait_ge(xh_ready, TC * n + t + 1)
                    cols = slice(t * P, (t + 1) * P)
                    nc.vector.tensor_tensor(xl[:, :, cols], banks[t % 2][:].rearrange("p (k c) -> p k c", k=KH),
                                            xh[:, :, cols].bitcast(F32), ALU.subtract).then_inc(xl_ready, 1)
                dve.wait_ge(rms_ready, n + 1)
                nc.vector.reciprocal(rrms[:], rms[:]).then_inc(rrms_ready, 1)
                dve.wait_ge(rrms_ready, n + 1)
                for t in range(TC):
                    nc.vector.tensor_scalar(qn[:, t, :], lat[:, t, 0:QL], rrms[:, 0, t:t + 1], None, ALU.mult).then_inc(qn_ready, 1)
                    for to in (0, KVL + ROPE):
                        op = nc.vector.tensor_scalar(kn[:, t, to:to + KVL], lat[:, t, QL:QL + KVL],
                                                     rrms[:, 1, t:t + 1], None, ALU.mult)
                    op.then_inc(cn_ready, 1)
                dve.wait_ge(cn_ready, TC * (n + 1))
                nc.vector.tensor_copy(c16[:, ds(TC * n, TC), 0, :], kn[:, :, 0:KVL]).then_inc(c16_hi, 1)
                dve.wait_ge(c16_hi, n + 1)
                nc.vector.tensor_tensor(c16[:, ds(TC * n, TC), 1, :], kn[:, :, 0:KVL], c16[:, ds(TC * n, TC), 0, :],
                                        ALU.subtract)
                for m in range(MT):
                    k = MT * n + m + 1
                    dve.wait_ge(exp_ready, k)
                    nc.vector.tensor_scalar(e1[:, m % 2, :], e1[:, m % 2, :], 1.0, None, ALU.add).then_inc(e1_ready, 1)
                    dve.wait_ge(e1_ready, k)
                    nc.vector.reciprocal(e1[:, m % 2, :], e1[:, m % 2, :]).then_inc(rec_ready, 1)
                    if m >= 1:
                        hidden_lo(n, m - 1)
                    dve.wait_ge(rec_ready, k)
                    nc.vector.scalar_tensor_tensor(out=e1[:, m % 2, :], in0=banks[4 + 2 * (m % 2)][:], scalar=b12[:, m:m + 1],
                                                   in1=e1[:, m % 2, :], op0=ALU.add, op1=ALU.mult).then_inc(g_ready, 1)
                    dve.wait_ge(g_ready, k)
                    nc.vector.scalar_tensor_tensor(out=hf[:, m % 2, :], in0=banks[5 + 2 * (m % 2)][:],
                                                   scalar=b12[:, MT + m:MT + m + 1], in1=e1[:, m % 2, :],
                                                   op0=ALU.add, op1=ALU.mult).then_inc(hf_ready, 1)
                hidden_lo(n, MT - 1)
                for t in range(TC):
                    dve.wait_ge(qkh_ready, TC * n + t + 1)
                    at = ds(TC * P * n + t * P, P)
                    nc.vector.tensor_tensor(qk_lo[:, :, at], qkf[:, t % 2], qk_hi[:, :, at].bitcast(F32),
                                            ALU.subtract).then_inc(qkl_ready, 1)
                dve.wait_ge(y_init, n + 1)
                for t in range(TC):
                    dve.wait_ge(down_mm, TC * n + t + 1)
                    nc.vector.tensor_tensor(x[:, t, :], banks[t % 2][:], x[:, t, :], ALU.add).then_inc(y_ready, 1)

        @block.tensor
        def _(pe):
            def three(out, terms):
                n = len(terms)
                for i, (lh, ll, rh, rl) in enumerate(terms):
                    nc.tensor.matmul(out, lh, rh, start=(i == 0), stop=False)
                    nc.tensor.matmul(out, lh, rl, start=False, stop=False)
                    mm = nc.tensor.matmul(out, ll, rh, start=False, stop=(i == n - 1))
                return mm

            pe.wait_ge(c_in, 16 * 9)
            pe.wait_ge(w_lo, NP)
            with pe.Fori(0, NCH) as n:
                for t in range(TC):
                    pe.wait_ge(xn_ready, TC * n + t + 1)
                    if t >= 2:
                        pe.wait_ge(xl_ready, TC * n + t - 1)
                    for k in range(KH):
                        mm = nc.tensor.transpose(banks[t % 2][:, k * P:(k + 1) * P], xn[:, t, k * P:(k + 1) * P], ident[:])
                    mm.then_inc(xt_mm, 1)
                for t in range(TC):
                    pe.wait_ge(xl_ready, TC * n + t + 1)
                    if t >= 2:
                        pe.wait_ge(lat_ready, TC * n + t - 1)
                    cols = slice(t * P, (t + 1) * P)
                    three(banks[2 + t % 2][:, 0:LAT],
                          [(xh[:, k, cols], xl[:, k, cols], wlh[:, k, :], wll[:, k, :]) for k in range(KH)]).then_inc(lat_mm, 1)
                for m in range(MT):
                    if m >= 2:
                        pe.wait_ge(hf_ready, MT * n + m - 1)
                    for half in range(2):
                        w = slice(half * FF + m * P, half * FF + (m + 1) * P)
                        mm = three(banks[4 + 2 * (m % 2) + half][:],
                                   [(w12h[:, k, w], w12l[:, k, w], xh[:, k, :], xl[:, k, :]) for k in range(KH)])
                    mm.then_inc(up_mm, 1)
                pe.wait_ge(qn_ready, TC * (n + 1))
                pe.wait_ge(cn_ready, TC * (n + 1))
                pe.wait_ge(rot_ready, n + 1)
                for t in range(TC):
                    if t >= 2:
                        pe.wait_ge(qkf_ready, TC * n + t - 1)
                    bank = banks[2 + t % 2]
                    nc.tensor.transpose(bank[:, 0:P], qn[:, t, 0:P], ident[:])
                    nc.tensor.transpose(bank[0:QL - P, P:2 * P], qn[:, t, P:QL], ident[:])
                    nc.tensor.transpose(bank[:, 2 * P:3 * P], kn[:, t, 0:KVL + ROPE], ident[:])
                    nc.tensor.transpose(bank[:, 3 * P:4 * P], kn[:, t, KVL:], ident[:]).then_inc(kt_mm, 1)
                pe.wait_ge(hl_ready, MT * (n + 1))
                for t in range(TC):
                    if t >= 2:
                        pe.wait_ge(y_ready, TC * n + t - 1)
                    cols = slice(t * P, (t + 1) * P)
                    three(banks[t % 2][:], [(hh[:, m, cols], hl[:, m, cols], w3h[:, m, :], w3l[:, m, :])
                                            for m in range(MT)]).then_inc(down_mm, 1)


def attention(nc, io, scr, res):
    qk_hi, qk_lo, c16 = res["qk_hi"], res["qk_lo"], res["c16"]
    ROUNDS = B * PAIRS // 2
    RPB = PAIRS // 2
    TPR = 4 * ST
    BLK = 4
    HALF = S // 512
    ORDER = [0, 7, 1, 6, 2, 5, 3, 4]
    groups = [-(-(i + 1) // BLK) for i in ORDER]
    GPH = sum(groups)
    gsum = lambda n: n // ST * GPH + sum(groups[:n % ST])
    GPR = gsum(TPR)
    with ExitStack() as ctx:
        sb = lambda n, s, d: ctx.enter_context(nc.sbuf_tensor(n + "_sb", s, d))
        sem = lambda n: ctx.enter_context(nc.semaphore(n))
        score = ctx.enter_context(nc.psum_tensor("score", [P, 4, 512], F32))
        flip = ctx.enter_context(nc.psum_tensor("flip", [P, 2, 512], F32))
        acc = ctx.enter_context(nc.psum_tensor("acc", [P, 512], F32))
        proj = ctx.enter_context(nc.psum_tensor("proj", [P, 512], F32))
        ident, mask = sb("ident2", [P, P], F32), sb("mask", [P, P], F32)
        ident_b, mask_b = sb("ident_b", [P, P], BF16), sb("mask_b", [P, P], BF16)
        cosT, sinT = sb("cosT", [P, 2, S], F32), sb("sinT", [P, S], F32)
        wh = [sb(f"wq_h{j}", [P, 2, 3 * P], F32R) for j in range(2)]
        wl = [sb(f"wq_l{j}", [P, 2, 3 * P], F32R) for j in range(2)]
        qh, ql = sb("qh", [P, 4, S], F32R), sb("ql", [P, 4, S], F32R)
        rot = sb("rot", [P, 2, 512], F32)
        qf = sb("qf", [P, 2, 2, 512], F32)
        prob = sb("prob", [P, 2, S], F32)
        pth, ptl = sb("pth", [P, 2, S], F16), sb("ptl", [P, 2, S], F16)
        shift, total = sb("shift", [P, TPR], F32), sb("total", [P, 4, ST], F32)
        rtot = sb("rtot", [P, 4, ST], F32)
        o = sb("o", [P, 2, ST, P], F32)
        const_in, w_in = sem("const_in"), [sem("wq_in0"), sem("wq_in1")]
        proj_mm, proj_out, rot_add, qh_ready, ql_ready = (
            sem(n) for n in ("proj_mm", "proj_out", "rot_add", "qh_ready", "ql_ready"))
        score_mm, shift_ready, exp_ready, flip_mm, pth_ready, ptl_ready, pv_mm, rtot_ready, o_ready = (
            sem(n) for n in ("score_mm", "shift_ready", "p_ready", "flip_mm", "pth_ready", "ptl_ready", "pv_mm", "rtot_ready", "o_ready"))
        o_out = [sem("o_out0"), sem("o_out1")]
        NCONST, cast_ready = 2, sem("cast_ready")
        PIECES = [(c, m) for c in range(HALF) for m in (2, 0, 1)]
        PIECE_AT = [0, 2, 3, 5, 7, 8]
        TAKE_AT = [1, 3, 4, 6, 8, 9]
        HI_AT = [4, 6, 9, 10]
        NPC = len(PIECES)
        o_dram = scr["o"].rearrange("(t p) c -> p t c", p=P)
        block = ctx.enter_context(nc.Block())

        def bank_of(pos):
            return 2 if pos % 2 else pos // 2 % 2

        @block.sync
        def _(sp):
            def load_w(j, pair):
                sp.dma_start(wh[j][:].rearrange("p k c -> p (k c)").bitcast(F32), scr["wq_hi"][:, ds(pair, 1), :]).then_inc(w_in[j], 16)
                sp.dma_start(wl[j][:].rearrange("p k c -> p (k c)").bitcast(F32), scr["wq_lo"][:, ds(pair, 1), :]).then_inc(w_in[j], 16)

            load_w(0, 0)
            for dst, src in ((sinT, "sinT"), (cosT, "cosT")):
                sp.dma_start(dst[:], io[src]).then_inc(const_in, 16)
            for j, (dst, src) in enumerate(((ident, "ident"), (mask, "mask"))):
                sp.dma_start(dst[:], io[src]).then_inc(o_out[j], 16)
            load_w(1, 1)
            sp.wait_ge(proj_mm, NPC)
            load_w(0, 2)
            with sp.Fori(0, ROUNDS) as it:
                b, pair = sp.snap(it // RPB), sp.snap((2 * it) % PAIRS)
                pair_b, pair_a = sp.snap((2 * it + 3) % PAIRS), sp.snap((2 * it + 4) % PAIRS)
                for j in range(2):
                    if j == 0:
                        sp.wait_ge(proj_mm, NPC * (2 * it + 2))
                        load_w(1, pair_b)
                    else:
                        sp.wait_ge(proj_mm, NPC * (2 * it + 3))
                        load_w(0, pair_a)
                    sp.wait_ge(o_ready, 4 * (2 * it + j + 1) + 1)
                    sp.dma_start(o_dram[:, ds(b * ST, ST), ds((pair + j) * P, P)], o[:, j]).then_inc(o_out[j], 16)
            sp.wait_ge(w_in[0], 32 * (ROUNDS + 2))
            sp.wait_ge(w_in[1], 32 * (ROUNDS + 1))
            for j in range(2):
                sp.wait_ge(o_out[j], 16 * (ROUNDS + 1))

        @block.tensor
        def _(pe):
            def project(k, piece, b, j):
                c, m = PIECES[piece]
                if piece == 0:
                    pe.wait_ge(w_in[j], k[1])
                if k[0] is not None:
                    pe.wait_ge(proj_out, k[0])
                cols = slice(m * P, (m + 1) * P)
                at = ds(b * S + c * 512, 512)
                for t in range(2):
                    rows = P if t == 0 else QL - P
                    for w, q in ((wh, qk_hi), (wh, qk_lo), (wl, qk_hi)):
                        mm = nc.tensor.matmul(proj[:], w[j][0:rows, t, cols], q[0:rows, t, at],
                                              start=(t == 0 and w is wh and q is qk_hi), stop=(t == 1 and w is wl))
                mm.then_inc(proj_mm, 1)

            def scores(n, b):
                n %= TPR
                head, pos = n // ST, n % ST
                i = ORDER[pos]
                kind = 2 + head % 2
                q = slice(i * P, (i + 1) * P)
                for c in range(groups[pos]):
                    w = min(BLK, i + 1 - BLK * c) * P
                    out = score[:, bank_of(pos) + c, 0:w]
                    at = ds(b * S + c * 512, w)
                    nc.tensor.matmul(out, qh[:, head, q], qk_hi[:, kind, at], start=True, stop=False)
                    if c == groups[pos] - 1:
                        nc.tensor.matmul(out[:, w - P:w], ident_b[:], mask_b[:], start=False, stop=False)
                    nc.tensor.matmul(out, qh[:, head, q], qk_lo[:, kind, at], start=False, stop=False)
                    mm = nc.tensor.matmul(out, ql[:, head, q], qk_hi[:, kind, at], start=False, stop=True)
                mm.then_inc(score_mm, 1)

            def transposes(n, tile, group):
                i = ORDER[n % ST]
                pe.wait_ge(exp_ready, tile + 1)
                for c in range(groups[n % ST]):
                    g = (gsum(n % TPR) + c) % 2
                    if n > 0:
                        pe.wait_ge(ptl_ready, group + c - (0 if n == 1 and c == 0 else 1))
                    for j in range(BLK * c, min(BLK * (c + 1), i + 1)):
                        mm = nc.tensor.transpose(flip[:, g, (j % BLK) * P:(j % BLK + 1) * P],
                                                 prob[:, n % 2, j * P:(j + 1) * P], ident[:])
                    mm.then_inc(flip_mm, 1)

            def values(n, b, tile, group, ogroup):
                pos = n % ST
                i = ORDER[pos]
                pe.wait_ge(ptl_ready, group + groups[pos])
                if pos % BLK == 0:
                    pe.wait_ge(o_ready, ogroup + 1)
                slot = sorted(ORDER[pos // BLK * BLK:][:BLK]).index(i)
                out = acc[:, slot * KVL:(slot + 1) * KVL]
                for j in range(i + 1):
                    p = slice(j * P, (j + 1) * P)
                    c = lambda half: c16[:, ds(b * ST + j, 1), half, :]
                    nc.tensor.matmul(out, pth[:, n % 2, p], c(0), start=(j == 0), stop=False)
                    nc.tensor.matmul(out, pth[:, n % 2, p], c(1), start=False, stop=False)
                    mm = nc.tensor.matmul(out, ptl[:, n % 2, p], c(0), start=False, stop=(j == i))
                mm.then_inc(pv_mm, 1)

            pe.wait_ge(cast_ready, 2)
            for piece in range(NPC):
                project((piece if piece else None, 32), piece, 0, 0)
            pe.wait_ge(ql_ready, 4)
            for n in range(3):
                scores(n, 0)
            transposes(0, 0, 0)
            with pe.Fori(0, ROUNDS) as it:
                b, b_next = it // RPB, ((it + 1) // RPB) % B
                for n in range(TPR):
                    transposes(n + 1, TPR * it + n + 1, GPR * it + gsum(n + 1))
                    if n + 3 in (TPR // 2, TPR):
                        pe.wait_ge(ql_ready, 8 * it + 4 + 4 * ((n + 3) // (TPR // 2)))
                    scores(n + 3, b if n + 3 < TPR else b_next)
                    values(n, b, TPR * it + n, GPR * it + gsum(n), TPR // BLK * it + n // BLK)
                    win, step = n // (TPR // 2), n % (TPR // 2)
                    if step in PIECE_AT:
                        piece = PIECE_AT.index(step)
                        k = NPC * (2 * it + 1 + win) + piece
                        if win == 0:
                            project((k, 32 * (it + 1)), piece, b, 1)
                        else:
                            project((k, 32 * (it + 2)), piece, b_next, 0)

        def nth(it, win, i, per, ahead):
            return per * (2 * it + win) + ahead + i + 1

        @block.scalar
        def _(act):
            def exp(n, tile):
                i = ORDER[n % ST]
                act.wait_ge(shift_ready, tile + 1)
                bank = bank_of(n % ST)
                src = score[:, bank:bank + groups[n % ST], :].rearrange("p b c -> p (b c)")[:, 0:(i + 1) * P]
                n %= TPR
                nc.scalar.activation(prob[:, n % 2, 0:(i + 1) * P], src, ACT.Exp, bias=shift[:, n:n + 1], scale=-1.0,
                                     accum_out=total[:, n // ST, i:i + 1]).then_inc(exp_ready, 1)

            def high(n, group):
                i = ORDER[n % ST]
                for c in range(groups[n % ST]):
                    act.wait_ge(flip_mm, group + c + 1)
                    w = min(BLK, i + 1 - BLK * c) * P
                    nc.scalar.activation(pth[:, n % 2, 512 * c:512 * c + w], flip[:, (gsum(n % TPR) + c) % 2, 0:w],
                                         ACT.Copy).then_inc(pth_ready, 1)

            def query_high(j, k, c, h):
                act.wait_ge(rot_add, k)
                nc.scalar.activation(qh[:, 2 * j + h, c * 512:(c + 1) * 512], qf[:, c, h, :], ACT.Copy).then_inc(qh_ready, 1)

            for k in range(4):
                query_high(0, k + 1, k // 2, k % 2)
            exp(0, 0)
            exp(1, 1)
            high(0, 0)
            with act.Fori(0, ROUNDS) as it:
                for n in range(TPR):
                    high(n + 1, GPR * it + gsum(n + 1))
                    exp(n + 2, TPR * it + n + 2)
                    win, step = n // (TPR // 2), n % (TPR // 2)
                    if step in HI_AT:
                        i = HI_AT.index(step)
                        query_high(1 - win, nth(it, win, i, 4, 4), i // 2, i % 2)

        @block.gpsimd
        def _(pool):
            def rotate(c, h, piece_count, done):
                if h == 1:
                    pool.wait_ge(rot_add, done + 1)
                elif done is not None:
                    pool.wait_ge(ql_ready, done)
                pool.wait_ge(proj_out, piece_count)
                rows = slice(KVL, P) if h == 0 else slice(0, ROPE)
                nc.gpsimd.tensor_tensor(qf[rows, c, h, :], qf[rows, c, h, :], rot[rows, c, :], ALU.add).then_inc(rot_add, 1)

            def query_low(j, c, h, k):
                pool.wait_ge(qh_ready, k)
                at = slice(c * 512, (c + 1) * 512)
                nc.gpsimd.tensor_tensor(ql[:, 2 * j + h, at], qf[:, c, h, :], qh[:, 2 * j + h, at].bitcast(F32),
                                        ALU.subtract).then_inc(ql_ready, 1)

            def pair(j, pieces, heads):
                for c in range(HALF):
                    for h in range(2):
                        first = isinstance(heads, int) and c == 0 and h == 0
                        rotate(c, h, pieces + 3 * c + 2 + h, None if first else heads + 2 * c)
                    for h in range(2):
                        query_low(j, c, h, heads + 2 * c + h + 1)

            pair(0, 0, 0)
            with pool.Fori(0, ROUNDS) as it:
                pair(1, NPC * (2 * it + 1), 4 * (2 * it + 1))
                pair(0, NPC * (2 * it + 2), 4 * (2 * it + 2))

        @block.vector
        def _(dve):
            def least(n, tile):
                i = ORDER[n % ST]
                dve.wait_ge(score_mm, tile + 1)
                bank = bank_of(n % ST)
                src = score[:, bank:bank + groups[n % ST], :].rearrange("p b c -> p (b c)")[:, 0:(i + 1) * P]
                n %= TPR
                nc.vector.tensor_reduce(shift[:, n:n + 1], src, AX.X, ALU.min).then_inc(shift_ready, 1)

            def low(n, group):
                i = ORDER[n % ST]
                for c in range(groups[n % ST]):
                    dve.wait_ge(pth_ready, group + c + 1)
                    w = min(BLK, i + 1 - BLK * c) * P
                    at = slice(512 * c, 512 * c + w)
                    nc.vector.tensor_tensor(ptl[:, n % 2, at], flip[:, (gsum(n % TPR) + c) % 2, 0:w], pth[:, n % 2, at],
                                            ALU.subtract).then_inc(ptl_ready, 1)

            def take(piece, k):
                c, m = PIECES[piece]
                dve.wait_ge(proj_mm, k)
                at = slice(c * 512, (c + 1) * 512)
                if m == 2:
                    op = nc.vector.tensor_tensor(rot[:, c, :], proj[:], sinT[:, at], ALU.mult)
                else:
                    op = nc.vector.tensor_tensor(qf[:, c, m, :], proj[:], cosT[:, m, at], ALU.mult)
                op.then_inc(proj_out, 1)

            def outputs(n, tile, ogroup, it):
                head, h = n // ST, n // ST % 2
                two = slice(0, 4, 3) if n % ST == BLK - 1 else slice(1, 3)
                by_two = lambda a: a.rearrange("p (a b) -> p a b", b=2)[:, two, :]
                dve.wait_ge(pv_mm, tile + 1)
                nc.vector.reciprocal(by_two(rtot[:, head]), by_two(total[:, head])).then_inc(rtot_ready, 1)
                dve.wait_ge(rtot_ready, ogroup + 1)
                if n % (TPR // 2) == BLK - 1:
                    dve.wait_ge(o_out[head // 2], 16 * (it + 1))
                nc.vector.tensor_tensor(
                    o[:, head // 2, :, h * KVL:(h + 1) * KVL].rearrange("p (a b) c -> p a b c", b=2)[:, two],
                    acc[:, 0:BLK * KVL].rearrange("p (a b c) -> p a b c", a=2, b=2),
                    by_two(rtot[:, head]).unsqueeze(3).broadcast_to([P, 2, 2, KVL]), ALU.mult).then_inc(o_ready, 1)

            nc.vector.memset(rtot[:], 0.0).then_inc(o_ready, 1)
            for j, (to, of) in enumerate(((ident_b, ident), (mask_b, mask))):
                dve.wait_ge(o_out[j], 16)
                nc.vector.tensor_copy(to[:], of[:]).then_inc(cast_ready, 1)
            dve.wait_ge(const_in, 16 * NCONST)
            for piece in range(NPC):
                take(piece, piece + 1)
            for n in range(3):
                least(n, n)
            low(0, 0)
            with dve.Fori(0, ROUNDS) as it:
                for n in range(TPR):
                    win, step = n // (TPR // 2), n % (TPR // 2)
                    if step in TAKE_AT:
                        piece = TAKE_AT.index(step)
                        take(piece, nth(it, win, piece, NPC, NPC))
                    low(n + 1, GPR * it + gsum(n + 1))
                    least(n + 3, TPR * it + n + 3)
                    if n % BLK == BLK - 1:
                        outputs(n, TPR * it + n, TPR // BLK * it + n // BLK, it)


def combine(nc, io, scr):
    NR = NT // 2
    with ExitStack() as ctx:
        sb = lambda n, s, d: ctx.enter_context(nc.sbuf_tensor(n + "_sb", s, d))
        sem = lambda n: ctx.enter_context(nc.semaphore(n))
        flip = [ctx.enter_context(nc.psum_tensor(f"turn{i}", [P, 512], F32)) for i in range(4)]
        acc = [ctx.enter_context(nc.psum_tensor(f"sum{i}", [P, 512], F32)) for i in range(2)]
        ident = sb("ident3", [P, P], F32)
        woh, wol = sb("woh", [P, PAIRS, H], F32R), sb("wol", [P, PAIRS, H], F32R)
        o = sb("o_nat", [P, 2, PAIRS * P], F32)
        oh, ol = sb("oT_hi", [P, 2, PAIRS, P], F32R), sb("oT_lo", [P, 2, PAIRS, P], F32R)
        y = sb("y_in", [P, 2, H], F32)
        in_w, in_t, in_y = sem("wo_in"), [sem("tile_in0"), sem("tile_in1")], [sem("y_in0"), sem("y_in1")]
        turn_mm, oh_ready, ol_ready, sum_mm, y_ready, stored = (
            sem(n) for n in ("turn_mm", "oh_ready", "ol_ready", "sum_mm", "sum_ready", "out_stored"))
        G = PAIRS // 4
        block = ctx.enter_context(nc.Block())

        @block.sync
        def _(sp):
            def load(t, j):
                sp.dma_start(o[:, j, :], scr["o"].rearrange("(t p) c -> p t c", p=P)[:, ds(t, 1), :]).then_inc(in_t[j], 16)

            sp.dma_start(ident[:], io["ident"]).then_inc(in_w, 16)
            load(0, 0)
            load(1, 1)
            for g in range(4):
                at = slice(g * PAIRS // 4, (g + 1) * PAIRS // 4)
                sp.dma_start(woh[:, at].bitcast(F32), scr["wo_hi"][:, at, :]).then_inc(in_w, 16)
                sp.dma_start(wol[:, at].bitcast(F32), scr["wo_lo"][:, at, :]).then_inc(in_w, 16)
            with sp.Fori(0, NR) as it:
                after = [sp.snap((2 * it + j + 2) % NT) for j in range(2)]
                for j in range(2):
                    sp.wait_ge(turn_mm, G * (2 * it + j + 1))
                    load(after[j], j)
            for j in range(2):
                sp.wait_ge(in_t[j], 16 * (NR + 1))

        @block.gpsimd
        def _(pool):
            def load(t, j):
                pool.dma_start(y[:, j, :], scr["y"][:, ds(t, 1), :]).then_inc(in_y[j], 16)

            load(0, 0)
            load(1, 1)
            with pool.Fori(0, NR) as it:
                after = [pool.snap((2 * it + j + 2) % NT) for j in range(2)]
                for j in range(2):
                    pool.wait_ge(y_ready, 2 * it + j + 1)
                    pool.dma_start(io["out"][:, ds(2 * it + j, 1), :], y[:, j:j + 1, :]).then_inc(stored, 16)
                    pool.wait_ge(stored, 16 * (2 * it + j + 1))
                    load(after[j], j)
            for j in range(2):
                pool.wait_ge(in_y[j], 16 * (NR + 1))

        @block.tensor
        def _(pe):
            def turn(j, tile, loads):
                pe.wait_ge(in_t[j], loads)
                for g in range(G):
                    if tile is not None:
                        pe.wait_ge(ol_ready, G * tile + g - G + 1)
                    for k in range(4):
                        pair = 4 * g + k
                        mm = nc.tensor.transpose(flip[g][:, k * P:(k + 1) * P], o[:, j, pair * P:(pair + 1) * P], ident[:])
                    mm.then_inc(turn_mm, 1)

            pe.wait_ge(in_w, 16 * 9)
            turn(0, None, 16)
            with pe.Fori(0, NR) as it:
                for j in range(2):
                    n = 2 * it + j
                    turn(1 - j, n + 1, 16 * (it + 1 + j))
                    pe.wait_ge(ol_ready, G * (n + 1))
                    for pair in range(PAIRS):
                        nc.tensor.matmul(acc[j][:], oh[:, j, pair, :], woh[:, pair, :], start=(pair == 0), stop=False)
                        nc.tensor.matmul(acc[j][:], oh[:, j, pair, :], wol[:, pair, :], start=False, stop=False)
                        mm = nc.tensor.matmul(acc[j][:], ol[:, j, pair, :], woh[:, pair, :], start=False,
                                              stop=(pair == PAIRS - 1))
                    mm.then_inc(sum_mm, 1)

        @block.scalar
        def _(act):
            def high(j, first):
                for g in range(G):
                    act.wait_ge(turn_mm, first + g + 1)
                    nc.scalar.activation(oh[:, j, 4 * g:4 * g + 4, :], flip[g][:].rearrange("p (k c) -> p k c", k=4),
                                         ACT.Copy).then_inc(oh_ready, 1)
            high(0, 0)
            with act.Fori(0, NR) as it:
                for j in range(2):
                    high(1 - j, G * (2 * it + j + 1))

        @block.vector
        def _(dve):
            def low(j, first):
                for g in range(G):
                    dve.wait_ge(oh_ready, first + g + 1)
                    at = slice(4 * g, 4 * g + 4)
                    nc.vector.tensor_tensor(ol[:, j, at, :], flip[g][:].rearrange("p (k c) -> p k c", k=4),
                                            oh[:, j, at, :].bitcast(F32), ALU.subtract).then_inc(ol_ready, 1)
            low(0, 0)
            with dve.Fori(0, NR) as it:
                for j in range(2):
                    low(1 - j, G * (2 * it + j + 1))
                    dve.wait_ge(sum_mm, 2 * it + j + 1)
                    dve.wait_ge(in_y[j], 16 * (it + 1))
                    nc.vector.tensor_tensor(y[:, j, :], acc[j][:], y[:, j, :], ALU.add).then_inc(y_ready, 1)


def build(nc, io):
    scr = {n: nc.dram_tensor(n, s, F32, kind="Internal").ap() for n, s in (
        ("y", (P, NT, H)), ("o", (TOK, PAIRS * P)), ("wq_hi", (P, PAIRS, WQ)), ("wq_lo", (P, PAIRS, WQ)),
        ("wo_hi", (P, PAIRS, H)), ("wo_lo", (P, PAIRS, H)))}
    absorb_weights(nc, io, scr)
    with ExitStack() as ctx:
        res = {n: ctx.enter_context(nc.sbuf_tensor(n, s, d)) for n, s, d in (
            ("qk_hi", [P, 4, TOK], F32R), ("qk_lo", [P, 4, TOK], F32R), ("c16", [P, NT, 2, KVL], F16))}
        dense(nc, io, scr, res)
        attention(nc, io, scr, res)
    combine(nc, io, scr)


def _tables():
    half = ROPE // 2
    expo = (np.arange(0, ROPE, 2, dtype=np.float32) / np.float32(ROPE)).astype(np.float64)
    freqs = np.float32(1.0) / (10000.0 ** expo).astype(np.float32)
    ang = np.outer(np.arange(S, dtype=np.float32), freqs).astype(np.float32)
    cos, sin = np.cos(ang).astype(np.float32), np.sin(ang).astype(np.float32)
    one = np.ones((KVL, S), np.float32)
    cosT = np.concatenate([cos.T, cos.T])
    rot = np.concatenate([-sin.T, sin.T])
    tok = lambda a: np.ascontiguousarray(a.reshape(ST, P, half).transpose(1, 0, 2))
    future = np.arange(P)[None, :] > np.arange(P)[:, None]
    return {
        "cos_tok": tok(cos), "sin_tok": tok(sin),
        "cosT": np.stack([np.concatenate([one, cosT]), np.concatenate([cosT, one])], 1),
        "sinT": np.concatenate([rot, rot]),
        "ident": np.eye(P, dtype=np.float32),
        "mask": np.where(future, 3.0e38, 0.0).astype(np.float32),
    }


def _layout(x):
    a = {k: np.asarray(v) for k, v in x.items()}
    half = ROPE // 2
    eo = np.concatenate([np.arange(0, ROPE, 2), np.arange(1, ROPE, 2)])
    oe = np.concatenate([eo[half:], eo[:half]])
    wqb = a["L0_attn_wq_b"].reshape(NH, NOPE + ROPE, QL)
    pe = wqb[:, NOPE:, :]
    pair = pe.reshape(PAIRS, 2, ROPE, QL)
    wqp = np.concatenate([pair[:, 0, eo], pair[:, 1, eo], pair[:, 1, oe], pair[:, 0, oe]], 1)
    wqp = wqp.transpose(2, 0, 1)
    wkva = a["L0_attn_wkv_a"]
    lat = np.concatenate([a["L0_attn_wq_a"], wkva[:KVL], wkva[KVL:][eo]], 0)
    wkvb = a["L0_attn_wkv_b"].reshape(NH, NOPE + VD, KVL)
    kt = lambda w: w.T.reshape(w.shape[1] // P, P, w.shape[0]).transpose(1, 0, 2)
    qnw, kvw = a["L0_attn_q_norm_w"], a["L0_attn_kv_norm_w"]
    col = lambda v: v.reshape(-1, P).T
    out = {
        "x": a["L0_attn_x"].reshape(NT, P, H).transpose(1, 0, 2),
        "wqn": wqb[:, :NOPE].transpose(1, 0, 2), "wqp0": wqp[:P], "wqp1": wqp[P:],
        "wk": wkvb[:, :NOPE].transpose(1, 0, 2), "wv": wkvb[:, NOPE:].transpose(1, 0, 2),
        "wo": a["L0_attn_wo"].T.reshape(NH, VD, H).transpose(1, 0, 2),
        "w_lat": kt(lat), "w12": kt(a["L0_ffn_w12"]), "w3": kt(a["L0_ffn_w3"]),
        "b12": col(a["L0_ffn_b12"]), "b3": a["L0_ffn_b3"].reshape(1, H),
        "qnw0": qnw[:P].reshape(P, 1), "qnw1": qnw[P:].reshape(QL - P, 1),
        "kvw": kvw.reshape(KVL, 1), "kvw2": np.concatenate([kvw, kvw]).reshape(P, 1),
        **_tables(),
    }
    return {k: np.ascontiguousarray(v) for k, v in out.items()}


def kernel(**inputs):
    import concourse.bacc as _bacc
    from concourse.bass_utils import run_bass_kernel_spmd as _run

    nc = _bacc.Bacc("TRN2", target_bir_lowering=False, num_devices=1)
    arrays = _layout(inputs)
    io = {k: nc.dram_tensor(k, v.shape, mybir.dt.from_np(v.dtype), kind="ExternalInput").ap()
          for k, v in arrays.items()}
    io["out"] = nc.dram_tensor("out", (P, NT, H), F32, kind="ExternalOutput").ap()
    build(nc, io)
    r = _run(nc, [arrays], core_ids=[0])
    return r.results[0]["out"].transpose(1, 0, 2).reshape(B, S, H)
```

```python
import numpy as np
from contextlib import ExitStack

import concourse.bass as bass
from concourse import mybir
from concourse.alu_op_type import AluOpType as ALU

ACT = mybir.ActivationFunctionType
AX = mybir.AxisListType
F32 = mybir.dt.float32
F32R = mybir.dt.float32r
F16 = mybir.dt.float16
BF16 = mybir.dt.bfloat16

P = 128
B, S, H = 2, 1024, 512
NH, NOPE, ROPE, VD = 32, 128, 64, 128
QL, KVL = 192, 64
FF = 512
TOK = B * S
NT = TOK // P
ST = S // P
KH = H // P
LAT = QL + KVL + ROPE
PAIRS = NH // 2
SCALE = 1.0 / float(np.sqrt(np.float32(NOPE + ROPE)))
LN_EPS, RMS_EPS = 1e-5, 1e-6
ds = bass.ds


def dense(nc, io, scr, res):
    qk_hi, qk_lo, c16 = res["qk_hi"], res["qk_lo"], res["c16"]
    TC = 4
    NCH = NT // TC
    MT = FF // P
    with ExitStack() as ctx:
        sb = lambda n, s, d: ctx.enter_context(nc.sbuf_tensor(n + "_sb", s, d))
        sem = lambda n: ctx.enter_context(nc.semaphore(n))
        banks = [ctx.enter_context(nc.psum_tensor(f"bank{i}", [P, 512], F32)) for i in range(8)]
        w12h, w12l = sb("w12h", [P, KH, 2 * FF], F32R), sb("w12l", [P, KH, 2 * FF], F32R)
        w3h, w3l = sb("w3h", [P, MT, H], F32R), sb("w3l", [P, MT, H], F32R)
        wlh, wll = sb("wlh", [P, KH, LAT], F32R), sb("wll", [P, KH, LAT], F32R)
        ident = sb("ident", [P, P], F32)
        b12 = sb("b12", [P, 2 * MT], F32)
        nb1 = sb("nb1", [P, MT], F32)
        b3 = sb("b3", [P, H], F32)
        cos, sin = sb("cos_tok", [P, ST, ROPE // 2], F32), sb("sin_tok", [P, ST, ROPE // 2], F32)
        wcol = sb("wcol", [P, 4], F32)
        scl = sb("scl", [P, 4], F32)
        eps = sb("eps", [P, 2], F32)
        x = sb("x", [P, TC, H], F32)
        xn = sb("xn", [P, TC, H], F32)
        stage = xn[:].rearrange("p t c -> p (t c)").rearrange("p (j c) -> p j c", j=2)
        st6, mv = sb("st6", [P, TC, 6], F32), sb("mv", [P, TC, 2], F32)
        fence = sb("fence", [P, 1], F32)
        sd, rsd = sb("sd", [P, TC], F32), sb("rsd", [P, TC], F32)
        xh, xl = sb("xh", [P, KH, TC * P], F32R), sb("xl", [P, KH, TC * P], F32R)
        lat = sb("lat", [P, TC, LAT], F32)
        junk = sb("junk", [P, TC, QL + KVL], BF16)
        ss, rms, rrms = sb("ss", [P, 2, TC], F32), sb("rms", [P, 2, TC], F32), sb("rrms", [P, 2, TC], F32)
        qn = sb("qn", [P, TC, 2 * P], F32)
        kn = sb("kn", [P, TC, KVL + ROPE + KVL], F32)
        rt = sb("rt", [P, 4, TC, ROPE // 2], F32)
        qkf = lat[:].rearrange("p t c -> p (t c)")[:, 0:8 * P].rearrange("p (j k c) -> p j k c", j=2, k=4)
        e1 = sb("e1", [P, 2, 512], F32)
        hf = sb("hf", [P, 2, 512], F32)
        hh, hl = sb("hh", [P, MT, 512], F32R), sb("hl", [P, MT, 512], F32R)

        w_in, w_hi, w_lo = [sem("w_in0"), sem("w_in1")], sem("w_hi"), sem("w_lo")
        c_in, c_set, c_ready = sem("c_in"), sem("c_set"), sem("c_ready")
        x_in, y_init = sem("x_in"), sem("y_init")
        stats, mv_ready, sd_ready, rsd_ready, xn_ready = sem("stats"), sem("mv_ready"), sem("sd_ready"), sem("rsd_ready"), sem("xn_ready")
        xt_mm, xh_ready, xl_ready = sem("xt_mm"), sem("xh_ready"), sem("xl_ready")
        lat_mm, ss_ready, lat_ready, rms_ready, rrms_ready = sem("lat_mm"), sem("ss_ready"), sem("lat_ready"), sem("rms_ready"), sem("rrms_ready")
        qn_ready, cn_ready, c16_hi, rot_mul, rot_ready = sem("qn_ready"), sem("cn_ready"), sem("c16_hi"), sem("rot_mul"), sem("rot_ready")
        kt_mm, qkf_ready, qkh_ready, qkl_ready = sem("kt_mm"), sem("qkf_ready"), sem("qkh_ready"), sem("qkl_ready")
        up_mm, exp_ready, e1_ready, rec_ready, g_ready, hf_ready, hh_ready, hl_ready = (
            sem(n) for n in ("up_mm", "exp_ready", "e1_ready", "rec_ready", "g_ready", "hf_ready", "hh_ready", "hl_ready"))
        down_mm, y_ready, y_out = sem("down_mm"), sem("y_ready"), sem("y_out")
        pieces = [("w12", k, 1, w12h, w12l) for k in range(KH)]
        pieces = [("w_lat", 0, 2, wlh, wll), ("w_lat", 2, 2, wlh, wll)] + pieces
        pieces += [("w3", 0, 2, w3h, w3l), ("w3", 2, 2, w3h, w3l)]
        NP = len(pieces)

        def staged(i):
            name, k, n, hi, lo = pieces[i]
            w = io[name].shape[2]
            return stage[:, i % 2, 0:n * w].rearrange("p (k c) -> p k c", k=n), hi[:, k:k + n, :], lo[:, k:k + n, :]

        block = ctx.enter_context(nc.Block())

        @block.sync
        def _(sp):
            sp.dma_start(x[:], io["x"][:, 0:TC, :]).then_inc(x_in, 16)
            sp.wait_ge(c_set, 1)
            for dst, src in ((ident[:], io["ident"]), (b12[:], io["b12"]), (b3[:], io["b3"].broadcast_to([P, H])),
                             (cos[:], io["cos_tok"]), (sin[:], io["sin_tok"]), (wcol[0:KVL, 0:1], io["kvw"]),
                             (wcol[ROPE:P, 1:2], io["kvw"]), (wcol[:, 2:3], io["qnw0"]), (wcol[:, 3:4], io["qnw1"])):
                sp.dma_start(dst, src).then_inc(c_in, 16)
            for i in range(NP):
                if i >= 2:
                    sp.wait_ge(w_lo, i - 1)
                name, k, n, _, _ = pieces[i]
                sp.dma_start(staged(i)[0], io[name][:, k:k + n, :]).then_inc(w_in[i % 2], 16)
            with sp.Fori(0, NCH - 1) as n:
                for t in range(TC):
                    sp.wait_ge(y_ready, TC * n + t + 1)
                    sp.dma_start(scr["y"][:, ds(TC * n + t, 1), :], x[:, t:t + 1, :]).then_inc(y_out, 16)
                sp.wait_ge(y_out, 16 * TC * (n + 1))
                sp.dma_start(x[:], io["x"][:, ds(TC * n + TC, TC), :]).then_inc(x_in, 16)
            for t in range(TC):
                sp.wait_ge(y_ready, TC * (NCH - 1) + t + 1)
                sp.dma_start(scr["y"][:, TC * (NCH - 1) + t, :], x[:, t, :]).then_inc(y_out, 16)
            sp.wait_ge(y_out, 16 * NT)

        @block.gpsimd
        def _(pool):
            pool.wait_ge(c_in, 16 * 9)
            half = ROPE // 2
            with pool.Fori(0, NCH) as n:
                pool.wait_ge(xn_ready, TC * (n + 1))
                for t in range(TC):
                    op = nc.gpsimd.tensor_tensor(x[:, t, :], x[:, t, :], b3[:], ALU.add)
                op.then_inc(y_init, 1)
                pool.wait_ge(lat_ready, TC * (n + 1))
                c = cos[:, ds(TC * (n % 2), TC), :]
                s = sin[:, ds(TC * (n % 2), TC), :]
                ev, od = lat[:, :, LAT - ROPE:LAT - half], lat[:, :, LAT - half:LAT]
                nc.gpsimd.tensor_tensor(rt[:, 0], ev, c, ALU.mult)
                nc.gpsimd.tensor_tensor(rt[:, 1], od, s, ALU.mult)
                nc.gpsimd.tensor_tensor(rt[:, 2], ev, s, ALU.mult)
                nc.gpsimd.tensor_tensor(rt[:, 3], od, c, ALU.mult).then_inc(rot_mul, 1)
                pool.wait_ge(rot_mul, n + 1)
                nc.gpsimd.tensor_tensor(kn[:, :, KVL:KVL + half], rt[:, 0], rt[:, 1], ALU.subtract)
                nc.gpsimd.tensor_tensor(kn[:, :, KVL + half:KVL + ROPE], rt[:, 2], rt[:, 3],
                                        ALU.add).then_inc(rot_ready, 1)

        @block.scalar
        def _(act):
            def split_weights(i):
                act.wait_ge(w_in[i % 2], 16 * (i // 2 + 1))
                src, hi, _ = staged(i)
                nc.scalar.activation(hi, src, ACT.Copy).then_inc(w_hi, 1)

            def up_exp(n, m):
                act.wait_ge(up_mm, MT * n + m + 1)
                nc.scalar.activation(e1[:, m % 2, :], banks[4 + 2 * (m % 2)][:], ACT.Exp, bias=nb1[:, m:m + 1],
                                     scale=-1.0).then_inc(exp_ready, 1)

            def hidden_hi(n, m):
                act.wait_ge(hf_ready, MT * n + m + 1)
                nc.scalar.activation(hh[:, m, :], hf[:, m % 2, :], ACT.Copy).then_inc(hh_ready, 1)

            for i in range(NP):
                split_weights(i)
            act.wait_ge(c_ready, 3)
            with act.Fori(0, NCH) as n:
                act.wait_ge(mv_ready, TC * (n + 1))
                nc.scalar.activation(sd[:], mv[:, :, 1], ACT.Sqrt, bias=eps[:, 0:1]).then_inc(sd_ready, 1)
                for t in range(TC):
                    act.wait_ge(xt_mm, TC * n + t + 1)
                    nc.scalar.activation(xh[:, :, t * P:(t + 1) * P],
                                         banks[t % 2][:].rearrange("p (k c) -> p k c", k=KH), ACT.Copy).then_inc(xh_ready, 1)
                for t in range(TC):
                    act.wait_ge(lat_mm, TC * n + t + 1)
                    bank = banks[2 + t % 2]
                    nc.scalar.activation(junk[:, t, 0:QL], bank[:, 0:QL], ACT.Square, accum_out=ss[:, 0, t:t + 1])
                    nc.scalar.activation(junk[:, t, QL:QL + KVL], bank[:, QL:QL + KVL], ACT.Square,
                                         accum_out=ss[:, 1, t:t + 1]).then_inc(ss_ready, 1)
                    nc.scalar.activation(lat[:, t, :], bank[:, 0:LAT], ACT.Copy).then_inc(lat_ready, 1)
                act.wait_ge(ss_ready, TC * (n + 1))
                nc.scalar.activation(rms[:, 0, :], ss[:, 0, :], ACT.Sqrt, bias=eps[:, 1:2], scale=1.0 / QL)
                nc.scalar.activation(rms[:, 1, :], ss[:, 1, :], ACT.Sqrt, bias=eps[:, 1:2],
                                     scale=1.0 / KVL).then_inc(rms_ready, 1)
                up_exp(n, 0)
                for m in range(1, MT):
                    up_exp(n, m)
                    hidden_hi(n, m - 1)
                hidden_hi(n, MT - 1)
                for t in range(TC):
                    act.wait_ge(kt_mm, TC * n + t + 1)
                    if t >= 2:
                        act.wait_ge(qkl_ready, TC * n + t - 1)
                    bank = banks[2 + t % 2]
                    for kind in range(4):
                        op = nc.scalar.activation(qkf[:, t % 2, kind, :], bank[:, kind * P:(kind + 1) * P],
                                                  ACT.Copy, scale=scl[:, kind:kind + 1])
                    op.then_inc(qkf_ready, 1)
                    act.wait_ge(qkf_ready, TC * n + t + 1)
                    nc.scalar.activation(qk_hi[:, :, ds(TC * P * n + t * P, P)], qkf[:, t % 2], ACT.Copy).then_inc(qkh_ready, 1)

        @block.vector
        def _(dve):
            nc.vector.memset(wcol[:], 1.0).then_inc(c_set, 1)
            nc.vector.memset(eps[:, 0:1], LN_EPS)
            nc.vector.memset(eps[:, 1:2], RMS_EPS)
            dve.wait_ge(c_in, 16 * 9)
            nc.vector.tensor_scalar(nb1[:], b12[:, 0:MT], -1.0, None, ALU.mult).then_inc(c_ready, 1)
            nc.vector.tensor_scalar(scl[:, 0:2], wcol[:, 0:2], -SCALE, None, ALU.mult).then_inc(c_ready, 1)
            nc.vector.tensor_copy(scl[:, 2:4], wcol[:, 2:4]).then_inc(c_ready, 1)
            for i in range(NP):
                dve.wait_ge(w_hi, i + 1)
                src, hi, lo = staged(i)
                nc.vector.tensor_tensor(lo, src, hi.bitcast(F32), ALU.subtract).then_inc(w_lo, 1)

            def hidden_lo(n, m):
                dve.wait_ge(hh_ready, MT * n + m + 1)
                nc.vector.tensor_tensor(hl[:, m, :], hf[:, m % 2, :], hh[:, m, :].bitcast(F32),
                                        ALU.subtract).then_inc(hl_ready, 1)

            with dve.Fori(0, NCH) as n:
                dve.wait_ge(x_in, 16 * (n + 1))
                for t in range(TC):
                    nc.vector.bn_stats(st6[:, t, :], x[:, t, :]).then_inc(stats, 1)
                dve.wait_ge(stats, TC * (n + 1))
                nc.vector.memset(fence[:], 0.0)
                for t in range(TC):
                    nc.vector.bn_aggr(mv[:, t, :], st6[:, t, :]).then_inc(mv_ready, 1)
                dve.wait_ge(sd_ready, n + 1)
                nc.vector.reciprocal(rsd[:], sd[:]).then_inc(rsd_ready, 1)
                dve.wait_ge(rsd_ready, n + 1)
                for t in range(TC):
                    nc.vector.tensor_scalar(xn[:, t, :], x[:, t, :], mv[:, t, 0:1], rsd[:, t:t + 1],
                                            ALU.subtract, ALU.mult).then_inc(xn_ready, 1)
                for t in range(TC):
                    dve.wait_ge(xh_ready, TC * n + t + 1)
                    cols = slice(t * P, (t + 1) * P)
                    nc.vector.tensor_tensor(xl[:, :, cols], banks[t % 2][:].rearrange("p (k c) -> p k c", k=KH),
                                            xh[:, :, cols].bitcast(F32), ALU.subtract).then_inc(xl_ready, 1)
                dve.wait_ge(rms_ready, n + 1)
                nc.vector.reciprocal(rrms[:], rms[:]).then_inc(rrms_ready, 1)
                dve.wait_ge(rrms_ready, n + 1)
                for t in range(TC):
                    nc.vector.tensor_scalar(qn[:, t, 0:QL], lat[:, t, 0:QL], rrms[:, 0, t:t + 1], None, ALU.mult)
                    nc.vector.tensor_scalar(qn[:, t, QL:2 * P], lat[:, t, P:QL], rrms[:, 0, t:t + 1], None,
                                            ALU.mult).then_inc(qn_ready, 1)
                    for to in (0, KVL + ROPE):
                        op = nc.vector.tensor_scalar(kn[:, t, to:to + KVL], lat[:, t, QL:QL + KVL],
                                                     rrms[:, 1, t:t + 1], None, ALU.mult)
                    op.then_inc(cn_ready, 1)
                dve.wait_ge(cn_ready, TC * (n + 1))
                nc.vector.tensor_copy(c16[:, ds(TC * n, TC), 0, :], kn[:, :, 0:KVL]).then_inc(c16_hi, 1)
                dve.wait_ge(c16_hi, n + 1)
                nc.vector.tensor_tensor(c16[:, ds(TC * n, TC), 1, :], kn[:, :, 0:KVL], c16[:, ds(TC * n, TC), 0, :],
                                        ALU.subtract)
                for m in range(MT):
                    k = MT * n + m + 1
                    dve.wait_ge(exp_ready, k)
                    nc.vector.tensor_scalar(e1[:, m % 2, :], e1[:, m % 2, :], 1.0, None, ALU.add).then_inc(e1_ready, 1)
                    dve.wait_ge(e1_ready, k)
                    nc.vector.reciprocal(e1[:, m % 2, :], e1[:, m % 2, :]).then_inc(rec_ready, 1)
                    if m >= 1:
                        hidden_lo(n, m - 1)
                    dve.wait_ge(rec_ready, k)
                    nc.vector.scalar_tensor_tensor(out=e1[:, m % 2, :], in0=banks[4 + 2 * (m % 2)][:], scalar=b12[:, m:m + 1],
                                                   in1=e1[:, m % 2, :], op0=ALU.add, op1=ALU.mult).then_inc(g_ready, 1)
                    dve.wait_ge(g_ready, k)
                    nc.vector.scalar_tensor_tensor(out=hf[:, m % 2, :], in0=banks[5 + 2 * (m % 2)][:],
                                                   scalar=b12[:, MT + m:MT + m + 1], in1=e1[:, m % 2, :],
                                                   op0=ALU.add, op1=ALU.mult).then_inc(hf_ready, 1)
                hidden_lo(n, MT - 1)
                for t in range(TC):
                    dve.wait_ge(qkh_ready, TC * n + t + 1)
                    at = ds(TC * P * n + t * P, P)
                    nc.vector.tensor_tensor(qk_lo[:, :, at], qkf[:, t % 2, 0:3], qk_hi[:, 0:3, at].bitcast(F32),
                                            ALU.subtract)
                    nc.vector.tensor_tensor(qk_hi[64:P, 3, at], qkf[64:P, t % 2, 3], qk_hi[64:P, 3, at].bitcast(F32),
                                            ALU.subtract).then_inc(qkl_ready, 1)
                dve.wait_ge(y_init, n + 1)
                for t in range(TC):
                    dve.wait_ge(down_mm, TC * n + t + 1)
                    nc.vector.tensor_tensor(x[:, t, :], banks[t % 2][:], x[:, t, :], ALU.add).then_inc(y_ready, 1)

        @block.tensor
        def _(pe):
            def three(out, terms):
                n = len(terms)
                for i, (lh, ll, rh, rl) in enumerate(terms):
                    nc.tensor.matmul(out, lh, rh, start=(i == 0), stop=False)
                    nc.tensor.matmul(out, lh, rl, start=False, stop=False)
                    mm = nc.tensor.matmul(out, ll, rh, start=False, stop=(i == n - 1))
                return mm

            pe.wait_ge(c_in, 16 * 9)
            pe.wait_ge(w_lo, NP)
            with pe.Fori(0, NCH) as n:
                for t in range(TC):
                    pe.wait_ge(xn_ready, TC * n + t + 1)
                    if t >= 2:
                        pe.wait_ge(xl_ready, TC * n + t - 1)
                    for k in range(KH):
                        mm = nc.tensor.transpose(banks[t % 2][:, k * P:(k + 1) * P], xn[:, t, k * P:(k + 1) * P], ident[:])
                    mm.then_inc(xt_mm, 1)
                for t in range(TC):
                    pe.wait_ge(xl_ready, TC * n + t + 1)
                    if t >= 2:
                        pe.wait_ge(lat_ready, TC * n + t - 1)
                    cols = slice(t * P, (t + 1) * P)
                    three(banks[2 + t % 2][:, 0:LAT],
                          [(xh[:, k, cols], xl[:, k, cols], wlh[:, k, :], wll[:, k, :]) for k in range(KH)]).then_inc(lat_mm, 1)
                for m in range(MT):
                    if m >= 2:
                        pe.wait_ge(hf_ready, MT * n + m - 1)
                    for half in range(2):
                        w = slice(half * FF + m * P, half * FF + (m + 1) * P)
                        mm = three(banks[4 + 2 * (m % 2) + half][:],
                                   [(w12h[:, k, w], w12l[:, k, w], xh[:, k, :], xl[:, k, :]) for k in range(KH)])
                    mm.then_inc(up_mm, 1)
                pe.wait_ge(qn_ready, TC * (n + 1))
                pe.wait_ge(cn_ready, TC * (n + 1))
                pe.wait_ge(rot_ready, n + 1)
                for t in range(TC):
                    if t >= 2:
                        pe.wait_ge(qkf_ready, TC * n + t - 1)
                    bank = banks[2 + t % 2]
                    nc.tensor.transpose(bank[:, 0:P], kn[:, t, 0:KVL + ROPE], ident[:])
                    nc.tensor.transpose(bank[:, P:2 * P], kn[:, t, KVL:], ident[:])
                    nc.tensor.transpose(bank[:, 2 * P:3 * P], qn[:, t, 0:P], ident[:])
                    nc.tensor.transpose(bank[:, 3 * P:4 * P], qn[:, t, P:2 * P], ident[:]).then_inc(kt_mm, 1)
                pe.wait_ge(hl_ready, MT * (n + 1))
                for t in range(TC):
                    if t >= 2:
                        pe.wait_ge(y_ready, TC * n + t - 1)
                    cols = slice(t * P, (t + 1) * P)
                    three(banks[t % 2][:], [(hh[:, m, cols], hl[:, m, cols], w3h[:, m, :], w3l[:, m, :])
                                            for m in range(MT)]).then_inc(down_mm, 1)


def attention(nc, io, scr, res):
    qk_hi, qk_lo, c16, wo_out = res["qk_hi"], res["qk_lo"], res["c16"], res["wo_out"]
    ROUNDS = B * PAIRS // 2
    RPB = PAIRS // 2
    BLK = 4
    HALF = S // 512
    CPH = ST // 2
    CPR = 4 * CPH
    WIN = CPR // 2
    GPC = 3
    SHORT, LONG = 0, 1
    with ExitStack() as ctx:
        sb = lambda n, s, d: ctx.enter_context(nc.sbuf_tensor(n + "_sb", s, d))
        sem = lambda n: ctx.enter_context(nc.semaphore(n))
        score = ctx.enter_context(nc.psum_tensor("score", [P, 4, 512], F32))
        flip = ctx.enter_context(nc.psum_tensor("flip", [P, 2, 512], F32))
        acc = ctx.enter_context(nc.psum_tensor("acc", [P, 512], F32))
        proj = ctx.enter_context(nc.psum_tensor("proj", [P, 512], F32))
        ident, mask = sb("ident2", [P, P], F32), sb("mask", [P, P], F32)
        ident_b, mask_b = sb("ident_b", [P, P], BF16), sb("mask_b", [P, P], BF16)
        cosT, sinT = sb("cosT", [P, 2, S], F32), sb("sinT", [P, S], F32)
        raw = [sb(f"wqk{j}", [P, 2, 2 * P + KVL], F32) for j in range(2)]
        wf = [sb(f"wq_f{j}", [P, 2, 2 * P], F32) for j in range(2)]
        wh = [sb(f"wq_h{j}", [P, 2, 2 * P], F32R) for j in range(2)]
        wl = [sb(f"wq_l{j}", [P, 2, 2 * P], F32R) for j in range(2)]
        qh, ql = sb("qh", [P, 4, S], F32R), sb("ql", [P, 4, S], F32R)
        rot = sb("rot", [P, 2, 512], F32)
        qf = sb("qf", [P, 2, 2, 512], F32)
        prob = [sb("prob_short", [P, 512], F32), sb("prob_long", [P, S], F32)]
        pth = [sb("pth_short", [P, 2, 512], F16), sb("pth_long", [P, 2, S], F16)]
        ptl = [sb("ptl_short", [P, 2, 512], F16), sb("ptl_long", [P, 2, S], F16)]
        shift, total = sb("shift", [P, CPR, 2], F32), sb("total", [P, 4, ST], F32)
        rtot = sb("rtot", [P, 4, ST], F32)
        o = sb("o", [P, 2, ST, P], F32)
        wv, wo, kvw2 = sb("wv", [P, 2, KVL], F32), sb("wo", [P, 2, H], F32), sb("kvw2", [P, 1], F32)
        wo_in, wo_mm, wo_ready = sem("wo_in"), sem("wo_mm"), sem("wo_ready")
        const_in, w_in = sem("const_in"), [sem("wq_in0"), sem("wq_in1")]
        proj_mm, proj_out, rot_add, qh_ready, ql_ready = (
            sem(n) for n in ("proj_mm", "proj_out", "rot_add", "qh_ready", "ql_ready"))
        score_mm, shift_ready, flip_mm, pth_ready, ptl_ready, pv_mm, rtot_ready, o_ready = (
            sem(n) for n in ("score_mm", "shift_ready", "flip_mm", "pth_ready", "ptl_ready", "pv_mm", "rtot_ready", "o_ready"))
        exp_ready = [sem("exp_short"), sem("exp_long")]
        o_out = [sem("o_out0"), sem("o_out1")]
        NCONST, cast_ready = 3, sem("cast_ready")
        absorb_mm, lat_ready, wh_ready, wl_ready = (sem(n) for n in ("absorb_mm", "wlat_ready", "wh_ready", "wl_ready"))
        rot_in, rot_mul = [sem("rot_in0"), sem("rot_in1")], sem("rot_mul")
        window = lambda m: divmod(m + 1, WIN)
        PIECES = [(c, h) for c in range(HALF) for h in range(2)]
        PIECE_AT = [(0, "middle"), (0, "end"), (1, "middle"), (1, "end")]
        TAKE_AT = [(0, "middle"), (1, "start"), (1, "middle"), (2, "start")]
        HI_AT = [3, 3, 4, 5]
        ABSORB_AT, LAT_AT, WH_AT, WL_AT = 3, 4, 5, 6
        WO_AT, WO_TAKE_AT = 5, 6
        NPC = len(PIECES)
        o_dram = scr["o"].rearrange("(t p) c -> p t c", p=P)
        block = ctx.enter_context(nc.Block())

        def tile(m, kind):
            m %= CPR
            return m // CPH, ST - 1 - m % CPH if kind == LONG else m % CPH

        def banks_of(m, kind):
            return (1 + m % 2, 2) if kind == LONG else (0, 1)

        def score_of(m, kind):
            first, n = banks_of(m, kind)
            return score[:, first:first + n, :].rearrange("p b c -> p (b c)")[:, 0:(tile(m, kind)[1] + 1) * P]

        def turned(m, kind, c):
            i = tile(m, kind)[1]
            g = c if kind == LONG else 2
            return g, (GPC * m + g) % 2, slice(512 * c, 512 * c + min(BLK, i + 1 - BLK * c) * P)

        @block.sync
        def _(sp):
            def load_w(j, pair):
                sp.dma_start(raw[j][:].rearrange("p h c -> p (h c)"), io["wqk"][:, ds(pair, 1), :]).then_inc(w_in[j], 16)
                sp.dma_start(wf[j][:, :, KVL:KVL + 2 * ROPE], io["wqp"][:, ds(pair, 1), :, :]).then_inc(w_in[j], 16)

            def load_wo(pair):
                heads = slice(2 * pair, 2 * pair + 2) if isinstance(pair, int) else ds(pair * 2, 2)
                sp.dma_start(wv[:], io["wv"][:, heads, :]).then_inc(wo_in, 16)
                sp.dma_start(wo[:], io["wo"][:, heads, :]).then_inc(wo_in, 16)

            def swap_halves(c, taken):
                sp.wait_ge(proj_out, taken)
                half = ROPE // 2
                for h, base in ((0, KVL), (1, 0)):
                    for to, of in ((base, base + half), (base + half, base)):
                        sp.dma_start(rot[to:to + half, c, :], qf[of:of + half, c, h, :]).then_inc(rot_in[c], 16)

            load_w(0, 0)
            load_w(1, 1)
            for dst, src in ((sinT, "sinT"), (cosT, "cosT"), (kvw2, "kvw2")):
                sp.dma_start(dst[:], io[src]).then_inc(const_in, 16)
            for j, (dst, src) in enumerate(((ident, "ident"), (mask, "mask"))):
                sp.dma_start(dst[:], io[src]).then_inc(o_out[j], 16)
            load_wo(0)
            for c in range(HALF):
                swap_halves(c, 2 * c + 2)
            for j in range(2):
                sp.wait_ge(wl_ready, j + 1)
                load_w(j, 2 + j)
            with sp.Fori(0, ROUNDS) as it:
                b, pair = sp.snap(it // RPB), sp.snap((2 * it) % PAIRS)
                next_wo = sp.snap((it + 1) % PAIRS)
                ahead = [sp.snap((2 * it + 4) % PAIRS), sp.snap((2 * it + 5) % PAIRS)]
                for j in range(2):
                    for c in range(HALF):
                        swap_halves(c, NPC * (2 * it + 1 + j) + 2 * c + 2)
                    sp.wait_ge(wl_ready, 2 * it + j + 3)
                    load_w(j, ahead[j])
                    if j == 0:
                        sp.wait_ge(wo_mm, it + 1)
                        load_wo(next_wo)
                    sp.wait_ge(o_ready, 4 * (2 * it + j + 1) + 1)
                    sp.dma_start(o_dram[:, ds(b * ST, ST), ds((pair + j) * P, P)], o[:, j]).then_inc(o_out[j], 16)
            for j in range(2):
                sp.wait_ge(w_in[j], 32 * (ROUNDS + 2))
                sp.wait_ge(wo_in, 32 * (ROUNDS + 1))
                sp.wait_ge(o_out[j], 16 * (ROUNDS + 1))

        @block.tensor
        def _(pe):
            def absorb(j, loads):
                pe.wait_ge(w_in[j], loads)
                for t in range(2):
                    for h in range(2):
                        at = slice(t * P + h * KVL, t * P + (h + 1) * KVL)
                        mm = nc.tensor.matmul(proj[:, at], raw[j][:, h, t * P:(t + 1) * P], raw[j][:, h, 2 * P:],
                                              start=True, stop=True)
                mm.then_inc(absorb_mm, 1)

            def project(piece, b, j):
                c, h = PIECES[piece]
                cols = slice(h * P, (h + 1) * P)
                at = ds(b * S + c * 512, 512)
                terms = ((wh, 0, qk_hi, 2), (wh, 0, qk_lo, 2), (wl, 0, qk_hi, 2), (wh, 1, qk_hi, 3), (wl, 1, qk_hi, 3))
                for i, (w, t, q, kind) in enumerate(terms):
                    mm = nc.tensor.matmul(proj[:], w[j][:, t, cols], q[:, kind, at], start=(i == 0), stop=(i == 4))
                mm.then_inc(proj_mm, 1)

            free_chunk, shared_chunk = lambda m: m % 2, lambda m: 1 - m % 2

            def scores(m, kind, b, c):
                head, i = tile(m, kind)
                keys = head % 2
                q = slice(i * P, (i + 1) * P)
                first, n = banks_of(m, kind)
                w = min(BLK, i + 1 - BLK * c) * P
                out = score[:, first + c, 0:w]
                at = ds(b * S + c * 512, w)
                nc.tensor.matmul(out, qh[:, head, q], qk_hi[:, keys, at], start=True, stop=False)
                nc.tensor.matmul(out, qh[:, head, q], qk_lo[:, keys, at], start=False, stop=False)
                last = c == n - 1
                mm = nc.tensor.matmul(out, ql[:, head, q], qk_hi[:, keys, at], start=False, stop=not last)
                if last:
                    mm = nc.tensor.matmul(out[:, w - P:w], ident_b[:], mask_b[:], start=False, stop=True)
                return mm

            def transposes(m, kind, before, c=0):
                g, bank, at = turned(m, kind, c)
                if before is not None:
                    pe.wait_ge(ptl_ready, before + g - 1)
                elif g == 2:
                    pe.wait_ge(ptl_ready, 1)
                for j in range(at.start // P, at.stop // P):
                    mm = nc.tensor.transpose(flip[:, bank, (j % BLK) * P:(j % BLK + 1) * P],
                                             prob[kind][:, j * P:(j + 1) * P], ident[:])
                mm.then_inc(flip_mm, 1)

            def values(m, kind, b):
                i = tile(m, kind)[1]
                slot = m % 2 if kind == SHORT else 3 - m % 2
                out = acc[:, slot * KVL:(slot + 1) * KVL]
                for j in range(i + 1):
                    p = slice(j * P, (j + 1) * P)
                    hi, lo = pth[kind][:, m % 2, p], ptl[kind][:, m % 2, p]
                    c = lambda half: c16[:, ds(b * ST + j, 1), half, :]
                    nc.tensor.matmul(out, hi, c(0), start=(j == 0), stop=False)
                    nc.tensor.matmul(out, hi, c(1), start=False, stop=False)
                    mm = nc.tensor.matmul(out, lo, c(0), start=False, stop=(j == i))
                return mm

            pe.wait_ge(cast_ready, 2)
            absorb(0, 32)
            pe.wait_ge(lat_ready, 1)
            absorb(1, 32)
            pe.wait_ge(wl_ready, 2)
            for piece in range(NPC):
                if piece:
                    pe.wait_ge(proj_out, piece)
                project(piece, 0, 0)
            pe.wait_ge(proj_out, NPC)
            project(0, 0, 1)
            pe.wait_ge(proj_out, NPC + 1)
            project(1, 0, 1)
            pe.wait_ge(ql_ready, 4)
            scores(0, LONG, 0, 0)
            scores(0, LONG, 0, 1).then_inc(score_mm, 1)
            scores(0, SHORT, 0, 0).then_inc(score_mm, 1)
            scores(1, LONG, 0, free_chunk(1))
            pe.wait_ge(exp_ready[LONG], 1)
            scores(1, LONG, 0, shared_chunk(1)).then_inc(score_mm, 1)
            transposes(0, LONG, None, 0)
            transposes(0, LONG, None, 1)
            pe.wait_ge(exp_ready[SHORT], 1)
            scores(1, SHORT, 0, 0).then_inc(score_mm, 1)
            scores(2, LONG, 0, free_chunk(2))
            transposes(0, SHORT, None)
            with pe.Fori(0, ROUNDS) as it:
                b, b_next = it // RPB, ((it + 1) // RPB) % B

                def extra(m, where):
                    win, step = window(m)
                    if (step, where) in PIECE_AT:
                        piece = PIECE_AT.index((step, where))
                        if piece:
                            pe.wait_ge(proj_out, NPC * (2 * it + 1 + win) + piece)
                        else:
                            pe.wait_ge(wl_ready, 2 * it + win + 2)
                            if win == 1:
                                pe.wait_ge(wo_ready, it + 1)
                        project(piece, b if win == 0 else b_next, 1 - win % 2)
                    if step == ABSORB_AT and where == "end":
                        pe.wait_ge(proj_out, NPC * (2 * it + 2 + win))
                        absorb(win, 32 * (it + 2))
                    if (win, step) == (0, WO_AT):
                        h = 0 if where == "middle" else 1
                        if h == 0:
                            pe.wait_ge(lat_ready, 2 * it + 3)
                            pe.wait_ge(wo_in, 32 * (it + 1))
                        mm = nc.tensor.matmul(proj[h * KVL:(h + 1) * KVL, :], wv[:, h, :], wo[:, h, :], start=True, stop=True)
                        if h == 1:
                            mm.then_inc(wo_mm, 1)

                for m in range(CPR):
                    done, banks = CPR * it + m, GPC * (CPR * it + m)
                    b_ahead = b if m + 2 < CPR else b_next
                    pe.wait_ge(exp_ready[LONG], done + 2)
                    scores(m + 2, LONG, b_ahead, shared_chunk(m)).then_inc(score_mm, 1)
                    transposes(m + 1, LONG, banks + GPC, 0)
                    transposes(m + 1, LONG, banks + GPC, 1)
                    pe.wait_ge(exp_ready[SHORT], done + 2)
                    scores(m + 2, SHORT, b_ahead, 0).then_inc(score_mm, 1)
                    pe.wait_ge(ptl_ready, banks + 2)
                    if m % 2 == 0:
                        pe.wait_ge(o_ready, CPR // 2 * it + m // 2 + 1)
                    values(m, LONG, b)
                    pe.wait_ge(ptl_ready, banks + GPC)
                    values(m, SHORT, b).then_inc(pv_mm, 1)
                    extra(m, "middle")
                    if (m + 3) % WIN == 0:
                        pe.wait_ge(ql_ready, 8 * it + 4 + 4 * ((m + 3) // WIN))
                    scores(m + 3, LONG, b if m + 3 < CPR else b_next, free_chunk(m + 1))
                    transposes(m + 1, SHORT, banks + GPC)
                    extra(m, "end")

        def nth(it, win, i, per, ahead):
            return per * (2 * it + win) + ahead + i + 1

        @block.scalar
        def _(act):
            def exp(m, kind, scored):
                head, i = tile(m, kind)
                act.wait_ge(shift_ready, scored)
                m %= CPR
                nc.scalar.activation(prob[kind][:, 0:(i + 1) * P], score_of(m, kind), ACT.Exp,
                                     bias=shift[:, m, kind:kind + 1], scale=-1.0,
                                     accum_out=total[:, head, i:i + 1]).then_inc(exp_ready[kind], 1)

            def high(m, kind, before, c=0):
                g, bank, at = turned(m, kind, c)
                act.wait_ge(flip_mm, before + g + 1)
                nc.scalar.activation(pth[kind][:, m % 2, at], flip[:, bank, 0:at.stop - at.start],
                                     ACT.Copy).then_inc(pth_ready, 1)

            def query_high(j, k, c, h):
                act.wait_ge(rot_add, k)
                nc.scalar.activation(qh[:, 2 * j + h, c * 512:(c + 1) * 512], qf[:, c, h, :], ACT.Copy).then_inc(qh_ready, 1)

            def take(piece, k):
                c, h = PIECES[piece]
                act.wait_ge(proj_mm, k)
                nc.scalar.activation(qf[:, c, h, :], proj[:], ACT.Copy).then_inc(proj_out, 1)

            def weights_latent(j, k):
                act.wait_ge(absorb_mm, k)
                for h, at in ((0, 0), (1, 2 * P - KVL)):
                    op = nc.scalar.activation(wf[j][:, :, at:at + KVL],
                                              proj[:, 0:2 * P].rearrange("p (t h c) -> p t h c", t=2, h=2)[:, :, h, :], ACT.Copy)
                op.then_inc(lat_ready, 1)

            def weights_high(j, k):
                act.wait_ge(lat_ready, k)
                nc.scalar.activation(wh[j][:], wf[j][:], ACT.Copy).then_inc(wh_ready, 1)

            act.wait_ge(const_in, 16 * NCONST)
            for j in range(2):
                weights_latent(j, j + 1)
                weights_high(j, j + 1)
            for piece in range(NPC):
                take(piece, piece + 1)
            for k in range(4):
                query_high(0, k + 1, k // 2, k % 2)
            act.wait_ge(ql_ready, 4)
            take(0, NPC + 1)
            exp(0, LONG, 1)
            exp(0, SHORT, 2)
            high(0, LONG, 0, 0)
            high(0, LONG, 0, 1)
            exp(1, LONG, 3)
            high(0, SHORT, 0)
            with act.Fori(0, ROUNDS) as it:
                def extra(m, where):
                    win, step = window(m)
                    if (step, where) in TAKE_AT:
                        piece = TAKE_AT.index((step, where))
                        if piece == 0:
                            act.wait_ge(ql_ready, 4 * (2 * it + win + 1))
                        take(piece, nth(it, win, piece, NPC, NPC))
                    if (win, step, where) == (0, WO_TAKE_AT, "middle"):
                        act.wait_ge(wo_mm, it + 1)
                        nc.scalar.activation(wo_out[:].bitcast(F32)[:, ds(it, 1), :], proj[:].rearrange("p (a c) -> p a c", a=1),
                                             ACT.Copy, scale=kvw2[:, 0:1]).then_inc(wo_ready, 1)
                    if where == "middle":
                        for i in range(4):
                            if HI_AT[i] == step:
                                query_high(1 - win, nth(it, win, i, 4, 4), i // 2, i % 2)
                    if where == "end":
                        if step == LAT_AT:
                            weights_latent(win, nth(it, win, 0, 1, 2))
                        if step == WH_AT:
                            weights_high(win, nth(it, win, 0, 1, 2))

                for m in range(CPR):
                    done, banks = CPR * it + m, GPC * (CPR * it + m)
                    extra(m, "start")
                    exp(m + 1, SHORT, 2 * done + 4)
                    high(m + 1, LONG, banks + GPC, 0)
                    high(m + 1, LONG, banks + GPC, 1)
                    exp(m + 2, LONG, 2 * done + 5)
                    extra(m, "middle")
                    high(m + 1, SHORT, banks + GPC)
                    extra(m, "end")

        @block.gpsimd
        def _(pool):
            def query_low(j, c, h, k):
                pool.wait_ge(qh_ready, k)
                at = slice(c * 512, (c + 1) * 512)
                nc.gpsimd.tensor_tensor(ql[:, 2 * j + h, at], qf[:, c, h, :], qh[:, 2 * j + h, at].bitcast(F32),
                                        ALU.subtract).then_inc(ql_ready, 1)

            def pair(j, before):
                for c in range(HALF):
                    at = slice(c * 512, (c + 1) * 512)
                    if c == 1:
                        pool.wait_ge(rot_add, 4 * before + 2)
                    pool.wait_ge(rot_in[c], 64 * (before + 1))
                    nc.gpsimd.tensor_tensor(rot[:, c, :], rot[:, c, :], sinT[:, at], ALU.mult)
                    for h in range(2):
                        op = nc.gpsimd.tensor_tensor(qf[:, c, h, :], qf[:, c, h, :], cosT[:, h, at], ALU.mult)
                    op.then_inc(rot_mul, 1)
                    pool.wait_ge(rot_mul, 2 * before + c + 1)
                    for h, rows in ((0, slice(KVL, P)), (1, slice(0, ROPE))):
                        if h == 1:
                            pool.wait_ge(rot_add, 4 * before + 2 * c + 1)
                        nc.gpsimd.tensor_tensor(qf[rows, c, h, :], qf[rows, c, h, :], rot[rows, c, :],
                                                ALU.add).then_inc(rot_add, 1)
                for c in range(HALF):
                    for h in range(2):
                        query_low(j, c, h, 4 * before + 2 * c + h + 1)

            pool.wait_ge(const_in, 16 * NCONST)
            pair(0, 0)
            with pool.Fori(0, ROUNDS) as it:
                pair(1, 2 * it + 1)
                pair(0, 2 * it + 2)

        @block.vector
        def _(dve):
            def least(m, kind, scored):
                dve.wait_ge(score_mm, scored)
                m %= CPR
                nc.vector.tensor_reduce(shift[:, m, kind:kind + 1], score_of(m, kind), AX.X, ALU.min).then_inc(shift_ready, 1)

            def low(m, kind, before, c=0):
                g, bank, at = turned(m, kind, c)
                dve.wait_ge(pth_ready, before + g + 1)
                nc.vector.tensor_tensor(ptl[kind][:, m % 2, at], flip[:, bank, 0:at.stop - at.start],
                                        pth[kind][:, m % 2, at], ALU.subtract).then_inc(ptl_ready, 1)

            def weights_low(j, k):
                dve.wait_ge(wh_ready, k)
                nc.vector.tensor_tensor(wl[j][:], wf[j][:], wh[j][:].bitcast(F32), ALU.subtract).then_inc(wl_ready, 1)

            def of_two(a, m):
                return a.rearrange("p (a b) -> p a b", b=2)[:, slice(0, 4, 3) if m % CPH < 2 else slice(1, 3), :]

            def inverse_sums(m):
                head = m // CPH
                nc.vector.reciprocal(of_two(rtot[:, head], m), of_two(total[:, head], m)).then_inc(rtot_ready, 1)

            def outputs(m, done, it):
                head, h = m // CPH, m // CPH % 2
                dve.wait_ge(pv_mm, done)
                dve.wait_ge(rtot_ready, CPR // 2 * it + m // 2 + 1)
                if m % WIN == 1:
                    dve.wait_ge(o_out[head // 2], 16 * (it + 1))
                two = slice(0, 4, 3) if m % CPH < 2 else slice(1, 3)
                nc.vector.tensor_tensor(
                    o[:, head // 2, :, h * KVL:(h + 1) * KVL].rearrange("p (a b) c -> p a b c", b=2)[:, two],
                    acc[:, 0:BLK * KVL].rearrange("p (a b c) -> p a b c", a=2, b=2),
                    of_two(rtot[:, head], m).unsqueeze(3).broadcast_to([P, 2, 2, KVL]), ALU.mult).then_inc(o_ready, 1)

            nc.vector.memset(rtot[:], 0.0).then_inc(o_ready, 1)
            for j, (to, of) in enumerate(((ident_b, ident), (mask_b, mask))):
                dve.wait_ge(o_out[j], 16)
                nc.vector.tensor_copy(to[:], of[:]).then_inc(cast_ready, 1)
            for j in range(2):
                weights_low(j, j + 1)
            least(0, LONG, 1)
            least(0, SHORT, 2)
            least(1, LONG, 3)
            low(0, LONG, 0, 0)
            low(0, LONG, 0, 1)
            least(1, SHORT, 4)
            low(0, SHORT, 0)
            with dve.Fori(0, ROUNDS) as it:
                for m in range(CPR):
                    done, banks = CPR * it + m, GPC * (CPR * it + m)
                    win, step = window(m)
                    if m % 2 == 1:
                        inverse_sums(m)
                    least(m + 2, LONG, 2 * done + 5)
                    low(m + 1, LONG, banks + GPC, 0)
                    low(m + 1, LONG, banks + GPC, 1)
                    least(m + 2, SHORT, 2 * done + 6)
                    low(m + 1, SHORT, banks + GPC)
                    if step == WL_AT:
                        weights_low(win, nth(it, win, 0, 1, 2))
                    if m % 2 == 1:
                        outputs(m, done + 1, it)


def combine(nc, io, scr, wol):
    NR = NT // 2
    with ExitStack() as ctx:
        sb = lambda n, s, d: ctx.enter_context(nc.sbuf_tensor(n + "_sb", s, d))
        sem = lambda n: ctx.enter_context(nc.semaphore(n))
        flip = [ctx.enter_context(nc.psum_tensor(f"turn{i}", [P, 512], F32)) for i in range(4)]
        acc = [ctx.enter_context(nc.psum_tensor(f"sum{i}", [P, 512], F32)) for i in range(2)]
        ident = sb("ident3", [P, P], F32)
        woh = sb("woh", [P, PAIRS, H], F32R)
        o = sb("o_nat", [P, 2, PAIRS * P], F32)
        oh, ol = sb("oT_hi", [P, 2, PAIRS, P], F32R), sb("oT_lo", [P, 2, PAIRS, P], F32R)
        y = sb("y_in", [P, 2, H], F32)
        woh_ready, wol_ready = sem("woh_ready"), sem("wol_ready")
        in_w, in_t, in_y = sem("ident_in"), [sem("tile_in0"), sem("tile_in1")], [sem("y_in0"), sem("y_in1")]
        turn_mm, oh_ready, ol_ready, sum_mm, y_ready, stored = (
            sem(n) for n in ("turn_mm", "oh_ready", "ol_ready", "sum_mm", "sum_ready", "out_stored"))
        G = PAIRS // 4
        block = ctx.enter_context(nc.Block())

        @block.sync
        def _(sp):
            def load(t, j):
                sp.dma_start(o[:, j, :], scr["o"].rearrange("(t p) c -> p t c", p=P)[:, ds(t, 1), :]).then_inc(in_t[j], 16)

            sp.dma_start(ident[:], io["ident"]).then_inc(in_w, 16)
            load(0, 0)
            load(1, 1)
            with sp.Fori(0, NR) as it:
                after = [sp.snap((2 * it + j + 2) % NT) for j in range(2)]
                for j in range(2):
                    sp.wait_ge(turn_mm, G * (2 * it + j + 1))
                    load(after[j], j)
            for j in range(2):
                sp.wait_ge(in_t[j], 16 * (NR + 1))

        @block.gpsimd
        def _(pool):
            def load(t, j):
                pool.dma_start(y[:, j, :], scr["y"][:, ds(t, 1), :]).then_inc(in_y[j], 16)

            load(0, 0)
            load(1, 1)
            with pool.Fori(0, NR) as it:
                after = [pool.snap((2 * it + j + 2) % NT) for j in range(2)]
                for j in range(2):
                    pool.wait_ge(y_ready, 2 * it + j + 1)
                    pool.dma_start(io["out"][:, ds(2 * it + j, 1), :], y[:, j:j + 1, :]).then_inc(stored, 16)
                    pool.wait_ge(stored, 16 * (2 * it + j + 1))
                    load(after[j], j)
            for j in range(2):
                pool.wait_ge(in_y[j], 16 * (NR + 1))

        @block.tensor
        def _(pe):
            def turn(j, tile, loads):
                pe.wait_ge(in_t[j], loads)
                for g in range(G):
                    if tile is not None:
                        pe.wait_ge(ol_ready, G * tile + g - G + 1)
                    for k in range(4):
                        pair = 4 * g + k
                        mm = nc.tensor.transpose(flip[g][:, k * P:(k + 1) * P], o[:, j, pair * P:(pair + 1) * P], ident[:])
                    mm.then_inc(turn_mm, 1)

            pe.wait_ge(in_w, 16)
            turn(0, None, 16)
            with pe.Fori(0, NR) as it:
                for j in range(2):
                    n = 2 * it + j
                    turn(1 - j, n + 1, 16 * (it + 1 + j))
                    pe.wait_ge(ol_ready, G * (n + 1))
                    for pair in range(PAIRS):
                        pe.wait_ge(wol_ready, pair + 1)
                        nc.tensor.matmul(acc[j][:], oh[:, j, pair, :], woh[:, pair, :], start=(pair == 0), stop=False)
                        nc.tensor.matmul(acc[j][:], oh[:, j, pair, :], wol[:, pair, :], start=False, stop=False)
                        mm = nc.tensor.matmul(acc[j][:], ol[:, j, pair, :], woh[:, pair, :], start=False,
                                              stop=(pair == PAIRS - 1))
                    mm.then_inc(sum_mm, 1)

        @block.scalar
        def _(act):
            def high(j, first):
                for g in range(G):
                    act.wait_ge(turn_mm, first + g + 1)
                    nc.scalar.activation(oh[:, j, 4 * g:4 * g + 4, :], flip[g][:].rearrange("p (k c) -> p k c", k=4),
                                         ACT.Copy).then_inc(oh_ready, 1)
            high(0, 0)
            for p in range(PAIRS):
                nc.scalar.activation(woh[:, p, :], wol[:, p, :].bitcast(F32), ACT.Copy).then_inc(woh_ready, 1)
            with act.Fori(0, NR) as it:
                for j in range(2):
                    high(1 - j, G * (2 * it + j + 1))

        @block.vector
        def _(dve):
            def low(j, first):
                for g in range(G):
                    dve.wait_ge(oh_ready, first + g + 1)
                    at = slice(4 * g, 4 * g + 4)
                    nc.vector.tensor_tensor(ol[:, j, at, :], flip[g][:].rearrange("p (k c) -> p k c", k=4),
                                            oh[:, j, at, :].bitcast(F32), ALU.subtract).then_inc(ol_ready, 1)
            low(0, 0)
            for p in range(PAIRS):
                dve.wait_ge(woh_ready, p + 1)
                nc.vector.tensor_tensor(wol[:, p, :], wol[:, p, :].bitcast(F32), woh[:, p, :].bitcast(F32),
                                        ALU.subtract).then_inc(wol_ready, 1)
            with dve.Fori(0, NR) as it:
                for j in range(2):
                    low(1 - j, G * (2 * it + j + 1))
                    dve.wait_ge(sum_mm, 2 * it + j + 1)
                    dve.wait_ge(in_y[j], 16 * (it + 1))
                    nc.vector.tensor_tensor(y[:, j, :], acc[j][:], y[:, j, :], ALU.add).then_inc(y_ready, 1)


def build(nc, io):
    scr = {n: nc.dram_tensor(n, s, F32, kind="Internal").ap() for n, s in (
        ("y", (P, NT, H)), ("o", (TOK, PAIRS * P)))}
    with ExitStack() as ctx:
        res = {n: ctx.enter_context(nc.sbuf_tensor(n, s, d)) for n, s, d in (
            ("qk_hi", [P, 4, TOK], F32R), ("qk_lo", [P, 3, TOK], F32R), ("c16", [P, NT, 2, KVL], F16))}
        dense(nc, io, scr, res)
        res["wo_out"] = ctx.enter_context(nc.sbuf_tensor("wo_out", [P, PAIRS, H], F32R))
        attention(nc, io, scr, res)
        combine(nc, io, scr, res["wo_out"])


def _tables():
    half = ROPE // 2
    expo = (np.arange(0, ROPE, 2, dtype=np.float32) / np.float32(ROPE)).astype(np.float64)
    freqs = np.float32(1.0) / (10000.0 ** expo).astype(np.float32)
    ang = np.outer(np.arange(S, dtype=np.float32), freqs).astype(np.float32)
    cos, sin = np.cos(ang).astype(np.float32), np.sin(ang).astype(np.float32)
    one = np.ones((KVL, S), np.float32)
    cosT = np.concatenate([cos.T, cos.T])
    rot = np.concatenate([-sin.T, sin.T])
    tok = lambda a: np.ascontiguousarray(a.reshape(ST, P, half).transpose(1, 0, 2))
    future = np.arange(P)[None, :] > np.arange(P)[:, None]
    return {
        "cos_tok": tok(cos), "sin_tok": tok(sin),
        "cosT": np.stack([np.concatenate([one, cosT]), np.concatenate([cosT, one])], 1),
        "sinT": np.concatenate([rot, rot]),
        "ident": np.eye(P, dtype=np.float32),
        "mask": np.where(future, 3.0e38, 0.0).astype(np.float32),
    }


def _layout(x):
    a = {k: np.asarray(v) for k, v in x.items()}
    half = ROPE // 2
    eo = np.concatenate([np.arange(0, ROPE, 2), np.arange(1, ROPE, 2)])
    wqb = a["L0_attn_wq_b"].reshape(NH, NOPE + ROPE, QL)
    pe = wqb[:, NOPE:, :]
    rows = np.concatenate([np.arange(QL), np.arange(P, QL)])
    wqp = pe[:, eo][:, :, rows].reshape(PAIRS, 2, ROPE, 2, P)
    wqp = wqp.transpose(4, 0, 3, 1, 2).reshape(P, PAIRS, 2, 2 * ROPE)
    wqn = wqb[:, :NOPE][:, :, rows].transpose(1, 0, 2)
    wkva = a["L0_attn_wkv_a"]
    lat = np.concatenate([a["L0_attn_wq_a"], wkva[:KVL], wkva[KVL:][eo]], 0)
    wkvb = a["L0_attn_wkv_b"].reshape(NH, NOPE + VD, KVL)
    kt = lambda w: w.T.reshape(w.shape[1] // P, P, w.shape[0]).transpose(1, 0, 2)
    qnw, kvw = a["L0_attn_q_norm_w"], a["L0_attn_kv_norm_w"]
    col = lambda v: v.reshape(-1, P).T
    out = {
        "x": a["L0_attn_x"].reshape(NT, P, H).transpose(1, 0, 2),
        "wqp": wqp,
        "wqk": np.concatenate([wqn, wkvb[:, :NOPE].transpose(1, 0, 2)], 2).reshape(P, PAIRS, 2 * (2 * P + KVL)),
        "wv": wkvb[:, NOPE:].transpose(1, 0, 2),
        "wo": a["L0_attn_wo"].T.reshape(NH, VD, H).transpose(1, 0, 2),
        "w_lat": kt(lat), "w12": kt(a["L0_ffn_w12"]), "w3": kt(a["L0_ffn_w3"]),
        "b12": col(a["L0_ffn_b12"]), "b3": a["L0_ffn_b3"].reshape(1, H),
        "qnw0": qnw[:P].reshape(P, 1), "qnw1": np.concatenate([qnw[P:], qnw[P:]]).reshape(P, 1),
        "kvw": kvw.reshape(KVL, 1), "kvw2": np.concatenate([kvw, kvw]).reshape(P, 1),
        **_tables(),
    }
    return {k: np.ascontiguousarray(v) for k, v in out.items()}


def kernel(**inputs):
    import concourse.bacc as _bacc
    from concourse.bass_utils import run_bass_kernel_spmd as _run

    nc = _bacc.Bacc("TRN2", target_bir_lowering=False, num_devices=1)
    arrays = _layout(inputs)
    io = {k: nc.dram_tensor(k, v.shape, mybir.dt.from_np(v.dtype), kind="ExternalInput").ap()
          for k, v in arrays.items()}
    io["out"] = nc.dram_tensor("out", (P, NT, H), F32, kind="ExternalOutput").ap()
    build(nc, io)
    r = _run(nc, [arrays], core_ids=[0])
    return r.results[0]["out"].transpose(1, 0, 2).reshape(B, S, H)
```

```python
import numpy as np
from contextlib import ExitStack

import concourse.bass as bass
from concourse import mybir
from concourse.alu_op_type import AluOpType as ALU

ACT = mybir.ActivationFunctionType
AX = mybir.AxisListType
F32 = mybir.dt.float32
F32R = mybir.dt.float32r
F16 = mybir.dt.float16
BF16 = mybir.dt.bfloat16

P = 128
B, S, H = 2, 1024, 512
NH, NOPE, ROPE, VD = 32, 128, 64, 128
QL, KVL = 192, 64
FF = 512
TOK = B * S
NT = TOK // P
ST = S // P
KH = H // P
LAT = QL + KVL + ROPE
PAIRS = NH // 2
SCALE = 1.0 / float(np.sqrt(np.float32(NOPE + ROPE)))
LN_EPS, RMS_EPS = 1e-5, 1e-6
ds = bass.ds


def dense(nc, io, scr, res):
    qk_hi, qk_lo, c16 = res["qk_hi"], res["qk_lo"], res["c16"]
    TC = 4
    NCH = NT // TC
    MT = FF // P
    with ExitStack() as ctx:
        sb = lambda n, s, d: ctx.enter_context(nc.sbuf_tensor(n + "_sb", s, d))
        sem = lambda n: ctx.enter_context(nc.semaphore(n))
        banks = [ctx.enter_context(nc.psum_tensor(f"bank{i}", [P, 512], F32)) for i in range(8)]
        w12h, w12l = sb("w12h", [P, KH, 2 * FF], F32R), sb("w12l", [P, KH, 2 * FF], F32R)
        w3h, w3l = sb("w3h", [P, MT, H], F32R), sb("w3l", [P, MT, H], F32R)
        wlh, wll = sb("wlh", [P, KH, LAT], F32R), sb("wll", [P, KH, LAT], F32R)
        ident = sb("ident", [P, P], F32)
        b12 = sb("b12", [P, 2 * MT], F32)
        b3 = sb("b3", [P, H], F32)
        cos, sin = sb("cos_tok", [P, ST, ROPE // 2], F32), sb("sin_tok", [P, ST, ROPE // 2], F32)
        wcol = sb("wcol", [P, 4], F32)
        scl = sb("scl", [P, 4], F32)
        eps = sb("eps", [P, 2], F32)
        x, xn = sb("x", [P, TC, H], F32), sb("xn", [P, TC, H], F32)
        y = sb("y", [P, TC, H], F32)
        stage = y[:].rearrange("p t c -> p (t c)").rearrange("p (j c) -> p j c", j=2)
        st6, mv = sb("st6", [P, TC, 6], F32), sb("mv", [P, TC, 2], F32)
        fence = sb("fence", [P, 1], F32)
        sd, rsd = sb("sd", [P, TC], F32), sb("rsd", [P, TC], F32)
        xh, xl = sb("xh", [P, KH, TC * P], F32R), sb("xl", [P, KH, TC * P], F32R)
        lat = sb("lat", [P, TC, LAT], F32)
        junk = sb("junk", [P, TC, QL + KVL], BF16)
        ss, rms, rrms = sb("ss", [P, 2, TC], F32), sb("rms", [P, 2, TC], F32), sb("rrms", [P, 2, TC], F32)
        qn = sb("qn", [P, TC, 2 * P], F32)
        kn = sb("kn", [P, TC, KVL + ROPE + KVL], F32)
        rt = sb("rt", [P, 4, TC, ROPE // 2], F32)
        qkf = lat[:].rearrange("p t c -> p (t c)")[:, 0:8 * P].rearrange("p (j k c) -> p j k c", j=2, k=4)
        gate = sb("gate", [P, 2, 512], F32)
        hf = sb("hf", [P, 2, 512], F32)
        hh, hl = sb("hh", [P, MT, 512], F32R), sb("hl", [P, MT, 512], F32R)

        w_in, w_hi, w_lo = [sem("w_in0"), sem("w_in1")], sem("w_hi"), sem("w_lo")
        c_in, c_set, c_ready = sem("c_in"), sem("c_set"), sem("c_ready")
        x_in, y_init = sem("x_in"), sem("y_init")
        stats, mv_ready, sd_ready, rsd_ready, xn_ready = sem("stats"), sem("mv_ready"), sem("sd_ready"), sem("rsd_ready"), sem("xn_ready")
        xt_mm, xh_ready, xl_ready = sem("xt_mm"), sem("xh_ready"), sem("xl_ready")
        lat_mm, ss_ready, lat_ready, rms_ready, rrms_ready = sem("lat_mm"), sem("ss_ready"), sem("lat_ready"), sem("rms_ready"), sem("rrms_ready")
        qn_ready, cn_ready, c16_hi, rot_mul, rot_ready = sem("qn_ready"), sem("cn_ready"), sem("c16_hi"), sem("rot_mul"), sem("rot_ready")
        kt_mm, qkf_ready, qkh_ready, qkl_ready = sem("kt_mm"), sem("qkf_ready"), sem("qkh_ready"), sem("qkl_ready")
        up_mm, gate_ready, hf_ready, hh_ready, hl_ready = (
            sem(n) for n in ("up_mm", "gate_ready", "hf_ready", "hh_ready", "hl_ready"))
        down_mm, y_ready, y_out = sem("down_mm"), sem("y_ready"), sem("y_out")
        pieces = [("w12", k, 1, w12h, w12l) for k in range(KH)]
        pieces = [("w_lat", 0, 2, wlh, wll), ("w_lat", 2, 2, wlh, wll)] + pieces
        pieces += [("w3", 0, 2, w3h, w3l), ("w3", 2, 2, w3h, w3l)]
        NP = len(pieces)
        NORM_AT = 1
        TURN_AT = {1: (0, 1), 2: (2, 3)}
        SPLIT_AT = {1: (0, 1)}
        SPLIT_LAST = (2, 3)
        NP_LAT, NP_UP = 2, 2 + KH

        def staged(i):
            name, k, n, hi, lo = pieces[i]
            w = io[name].shape[2]
            return stage[:, i % 2, 0:n * w].rearrange("p (k c) -> p k c", k=n), hi[:, k:k + n, :], lo[:, k:k + n, :]

        block = ctx.enter_context(nc.Block())

        @block.sync
        def _(sp):
            sp.dma_start(x[:], io["x"][:, 0:TC, :]).then_inc(x_in, 16)
            sp.dma_start(ident[:], io["ident"]).then_inc(y_out, 16)
            sp.wait_ge(c_set, 1)
            for dst, src in ((b12[:], io["b12"]), (b3[:], io["b3"].broadcast_to([P, H])),
                             (cos[:], io["cos_tok"]), (sin[:], io["sin_tok"]), (wcol[0:KVL, 0:1], io["kvw"]),
                             (wcol[ROPE:P, 1:2], io["kvw"]), (wcol[:, 2:3], io["qnw0"]), (wcol[:, 3:4], io["qnw1"])):
                sp.dma_start(dst, src).then_inc(c_in, 16)
            for i in range(NP):
                if i >= 2:
                    sp.wait_ge(w_lo, i - 1)
                name, k, n, _, _ = pieces[i]
                sp.dma_start(staged(i)[0], io[name][:, k:k + n, :]).then_inc(w_in[i % 2], 16)
            with sp.Fori(0, NCH - 1) as n:
                sp.wait_ge(xn_ready, TC * (n + 1))
                sp.wait_ge(y_init, n + 1)
                sp.dma_start(x[:], io["x"][:, ds(TC * n + TC, TC), :]).then_inc(x_in, 16)
                for t in range(TC):
                    sp.wait_ge(y_ready, TC * n + t + 1)
                    sp.dma_start(scr["y"][:, ds(TC * n + t, 1), :], y[:, t:t + 1, :]).then_inc(y_out, 16)
            for t in range(TC):
                sp.wait_ge(y_ready, TC * (NCH - 1) + t + 1)
                sp.dma_start(scr["y"][:, TC * (NCH - 1) + t, :], y[:, t, :]).then_inc(y_out, 16)
            sp.wait_ge(y_out, 16 * (NT + 1))

        @block.gpsimd
        def _(pool):
            pool.wait_ge(c_in, 16 * 8)
            half = ROPE // 2
            with pool.Fori(0, NCH) as n:
                pool.wait_ge(lat_ready, TC * (n + 1))
                c = cos[:, ds(TC * (n % 2), TC), :]
                s = sin[:, ds(TC * (n % 2), TC), :]
                ev, od = lat[:, :, LAT - ROPE:LAT - half], lat[:, :, LAT - half:LAT]
                nc.gpsimd.tensor_tensor(rt[:, 0], ev, c, ALU.mult)
                nc.gpsimd.tensor_tensor(rt[:, 1], od, s, ALU.mult)
                nc.gpsimd.tensor_tensor(rt[:, 2], ev, s, ALU.mult)
                nc.gpsimd.tensor_tensor(rt[:, 3], od, c, ALU.mult).then_inc(rot_mul, 1)
                pool.wait_ge(rot_mul, n + 1)
                nc.gpsimd.tensor_tensor(kn[:, :, KVL:KVL + half], rt[:, 0], rt[:, 1], ALU.subtract)
                nc.gpsimd.tensor_tensor(kn[:, :, KVL + half:KVL + ROPE], rt[:, 2], rt[:, 3],
                                        ALU.add).then_inc(rot_ready, 1)
                pool.wait_ge(w_lo, NP)
                pool.wait_ge(y_out, 16 * (TC * n + 1))
                for t in range(TC):
                    op = nc.gpsimd.tensor_tensor(y[:, t, :], x[:, t, :], b3[:], ALU.add)
                op.then_inc(y_init, 1)

        @block.scalar
        def _(act):
            def split_weights(i):
                act.wait_ge(w_in[i % 2], 16 * (i // 2 + 1))
                src, hi, _ = staged(i)
                nc.scalar.activation(hi, src, ACT.Copy).then_inc(w_hi, 1)

            def norm_root(n):
                act.wait_ge(mv_ready, TC * (n + 1))
                nc.scalar.activation(sd[:], mv[:, :, 1], ACT.Sqrt, bias=eps[:, 0:1]).then_inc(sd_ready, 1)

            def input_hi(n):
                for t in range(TC):
                    act.wait_ge(xt_mm, TC * n + t + 1)
                    nc.scalar.activation(xh[:, :, t * P:(t + 1) * P],
                                         banks[t % 2][:].rearrange("p (k c) -> p k c", k=KH), ACT.Copy).then_inc(xh_ready, 1)

            def latents(n):
                for t in range(TC):
                    act.wait_ge(lat_mm, TC * n + t + 1)
                    bank = banks[2 + t % 2]
                    nc.scalar.activation(junk[:, t, 0:QL], bank[:, 0:QL], ACT.Square, accum_out=ss[:, 0, t:t + 1])
                    nc.scalar.activation(junk[:, t, QL:QL + KVL], bank[:, QL:QL + KVL], ACT.Square,
                                         accum_out=ss[:, 1, t:t + 1]).then_inc(ss_ready, 1)
                    nc.scalar.activation(lat[:, t, :], bank[:, 0:LAT], ACT.Copy).then_inc(lat_ready, 1)
                act.wait_ge(ss_ready, TC * (n + 1))
                nc.scalar.activation(rms[:, 0, :], ss[:, 0, :], ACT.Sqrt, bias=eps[:, 1:2], scale=1.0 / QL)
                nc.scalar.activation(rms[:, 1, :], ss[:, 1, :], ACT.Sqrt, bias=eps[:, 1:2],
                                     scale=1.0 / KVL).then_inc(rms_ready, 1)

            def up_gate(n, m):
                act.wait_ge(up_mm, MT * n + m + 1)
                nc.scalar.activation(gate[:, m % 2, :], banks[4 + 2 * (m % 2)][:], ACT.Silu,
                                     bias=b12[:, m:m + 1]).then_inc(gate_ready, 1)

            def hidden_hi(n, m):
                act.wait_ge(hf_ready, MT * n + m + 1)
                nc.scalar.activation(hh[:, m, :], hf[:, m % 2, :], ACT.Copy).then_inc(hh_ready, 1)

            def latents_hi(n, tiles):
                for t in tiles:
                    act.wait_ge(kt_mm, TC * n + t + 1)
                    if t >= 2:
                        act.wait_ge(qkl_ready, TC * n + t - 1)
                    bank = banks[2 + t % 2]
                    for kind in range(4):
                        op = nc.scalar.activation(qkf[:, t % 2, kind, :], bank[:, kind * P:(kind + 1) * P],
                                                  ACT.Copy, scale=scl[:, kind:kind + 1])
                    op.then_inc(qkf_ready, 1)
                    act.wait_ge(qkf_ready, TC * n + t + 1)
                    nc.scalar.activation(qk_hi[:, :, ds(TC * P * n + t * P, P)], qkf[:, t % 2], ACT.Copy).then_inc(qkh_ready, 1)

            def chunk(n, more):
                for m in range(MT):
                    up_gate(n, m)
                    if m >= 1:
                        hidden_hi(n, m - 1)
                    latents_hi(n, SPLIT_AT.get(m, ()))
                    if m == NORM_AT and more:
                        norm_root(n + 1)
                hidden_hi(n, MT - 1)
                if more:
                    input_hi(n + 1)
                latents_hi(n, SPLIT_LAST)
                if more:
                    act.wait_ge(qkl_ready, TC * (n + 1))
                    latents(n + 1)

            act.wait_ge(c_ready, 2)
            norm_root(0)
            for i in range(NP_LAT):
                split_weights(i)
            input_hi(0)
            for i in range(NP_LAT, NP_UP):
                split_weights(i)
            latents(0)
            for i in range(NP_UP, NP):
                split_weights(i)
            with act.Fori(0, NCH - 1) as n:
                chunk(n, True)
            chunk(NCH - 1, False)

        @block.vector
        def _(dve):
            nc.vector.memset(wcol[:], 1.0).then_inc(c_set, 1)
            nc.vector.memset(eps[:, 0:1], LN_EPS)
            nc.vector.memset(eps[:, 1:2], RMS_EPS)
            dve.wait_ge(c_in, 16 * 8)
            nc.vector.tensor_scalar(scl[:, 0:2], wcol[:, 0:2], -SCALE, None, ALU.mult).then_inc(c_ready, 1)
            nc.vector.tensor_copy(scl[:, 2:4], wcol[:, 2:4]).then_inc(c_ready, 1)

            def split_weights(i):
                dve.wait_ge(w_hi, i + 1)
                src, hi, lo = staged(i)
                nc.vector.tensor_tensor(lo, src, hi.bitcast(F32), ALU.subtract).then_inc(w_lo, 1)

            def layer_norm(n):
                dve.wait_ge(x_in, 16 * (n + 1))
                for t in range(TC):
                    nc.vector.bn_stats(st6[:, t, :], x[:, t, :]).then_inc(stats, 1)
                dve.wait_ge(stats, TC * (n + 1))
                nc.vector.memset(fence[:], 0.0)
                for t in range(TC):
                    nc.vector.bn_aggr(mv[:, t, :], st6[:, t, :]).then_inc(mv_ready, 1)
                dve.wait_ge(sd_ready, n + 1)
                nc.vector.reciprocal(rsd[:], sd[:]).then_inc(rsd_ready, 1)
                dve.wait_ge(rsd_ready, n + 1)
                for t in range(TC):
                    nc.vector.tensor_scalar(xn[:, t, :], x[:, t, :], mv[:, t, 0:1], rsd[:, t:t + 1],
                                            ALU.subtract, ALU.mult).then_inc(xn_ready, 1)

            def input_lo(n):
                for t in range(TC):
                    dve.wait_ge(xh_ready, TC * n + t + 1)
                    cols = slice(t * P, (t + 1) * P)
                    nc.vector.tensor_tensor(xl[:, :, cols], banks[t % 2][:].rearrange("p (k c) -> p k c", k=KH),
                                            xh[:, :, cols].bitcast(F32), ALU.subtract).then_inc(xl_ready, 1)

            def latents(n):
                dve.wait_ge(rms_ready, n + 1)
                nc.vector.reciprocal(rrms[:], rms[:]).then_inc(rrms_ready, 1)
                dve.wait_ge(rrms_ready, n + 1)
                for t in range(TC):
                    nc.vector.tensor_scalar(qn[:, t, 0:QL], lat[:, t, 0:QL], rrms[:, 0, t:t + 1], None, ALU.mult)
                    nc.vector.tensor_scalar(qn[:, t, QL:2 * P], lat[:, t, P:QL], rrms[:, 0, t:t + 1], None,
                                            ALU.mult).then_inc(qn_ready, 1)
                    for to in (0, KVL + ROPE):
                        op = nc.vector.tensor_scalar(kn[:, t, to:to + KVL], lat[:, t, QL:QL + KVL],
                                                     rrms[:, 1, t:t + 1], None, ALU.mult)
                    op.then_inc(cn_ready, 1)
                dve.wait_ge(cn_ready, TC * (n + 1))
                nc.vector.tensor_copy(c16[:, ds(TC * n, TC), 0, :], kn[:, :, 0:KVL]).then_inc(c16_hi, 1)
                dve.wait_ge(c16_hi, n + 1)
                nc.vector.tensor_tensor(c16[:, ds(TC * n, TC), 1, :], kn[:, :, 0:KVL], c16[:, ds(TC * n, TC), 0, :],
                                        ALU.subtract)

            def hidden(n, m):
                if m >= 2:
                    dve.wait_ge(hl_ready, MT * n + m - 1)
                dve.wait_ge(gate_ready, MT * n + m + 1)
                nc.vector.scalar_tensor_tensor(out=hf[:, m % 2, :], in0=banks[5 + 2 * (m % 2)][:],
                                               scalar=b12[:, MT + m:MT + m + 1], in1=gate[:, m % 2, :],
                                               op0=ALU.add, op1=ALU.mult).then_inc(hf_ready, 1)

            def hidden_lo(n, m):
                dve.wait_ge(hh_ready, MT * n + m + 1)
                nc.vector.tensor_tensor(hl[:, m, :], hf[:, m % 2, :], hh[:, m, :].bitcast(F32),
                                        ALU.subtract).then_inc(hl_ready, 1)

            def latents_lo(n, tiles):
                for t in tiles:
                    dve.wait_ge(qkh_ready, TC * n + t + 1)
                    at = ds(TC * P * n + t * P, P)
                    nc.vector.tensor_tensor(qk_lo[:, :, at], qkf[:, t % 2, 0:3], qk_hi[:, 0:3, at].bitcast(F32),
                                            ALU.subtract)
                    nc.vector.tensor_tensor(qk_hi[64:P, 3, at], qkf[64:P, t % 2, 3], qk_hi[64:P, 3, at].bitcast(F32),
                                            ALU.subtract).then_inc(qkl_ready, 1)

            def chunk(n, more):
                latents(n)
                for m in range(MT):
                    hidden(n, m)
                    if m >= 1:
                        hidden_lo(n, m - 1)
                    latents_lo(n, SPLIT_AT.get(m, ()))
                    if m == NORM_AT and more:
                        layer_norm(n + 1)
                hidden_lo(n, MT - 1)
                if more:
                    input_lo(n + 1)
                latents_lo(n, SPLIT_LAST)
                dve.wait_ge(y_init, n + 1)
                for t in range(TC):
                    dve.wait_ge(down_mm, TC * n + t + 1)
                    nc.vector.tensor_tensor(y[:, t, :], banks[4 + t][:], y[:, t, :], ALU.add).then_inc(y_ready, 1)

            layer_norm(0)
            for i in range(NP_LAT):
                split_weights(i)
            input_lo(0)
            for i in range(NP_LAT, NP):
                split_weights(i)
            with dve.Fori(0, NCH - 1) as n:
                chunk(n, True)
            chunk(NCH - 1, False)

        @block.tensor
        def _(pe):
            def three(out, terms):
                n = len(terms)
                for i, (lh, ll, rh, rl) in enumerate(terms):
                    nc.tensor.matmul(out, lh, rh, start=(i == 0), stop=False)
                    nc.tensor.matmul(out, lh, rl, start=False, stop=False)
                    mm = nc.tensor.matmul(out, ll, rh, start=False, stop=(i == n - 1))
                return mm

            def turn_input(n):
                for t in range(TC):
                    pe.wait_ge(xn_ready, TC * n + t + 1)
                    if t >= 2:
                        pe.wait_ge(xl_ready, TC * n + t - 1)
                    for k in range(KH):
                        mm = nc.tensor.transpose(banks[t % 2][:, k * P:(k + 1) * P], xn[:, t, k * P:(k + 1) * P], ident[:])
                    mm.then_inc(xt_mm, 1)

            def latents(n, sums_before):
                for t in range(TC):
                    pe.wait_ge(xl_ready, TC * n + t + 1)
                    if t >= 2:
                        pe.wait_ge(lat_ready, TC * n + t - 1)
                    if t == TC - 1 and sums_before is not None:
                        pe.wait_ge(y_ready, sums_before)
                    cols = slice(t * P, (t + 1) * P)
                    three(banks[2 + t % 2][:, 0:LAT],
                          [(xh[:, k, cols], xl[:, k, cols], wlh[:, k, :], wll[:, k, :]) for k in range(KH)]).then_inc(lat_mm, 1)

            def turn_latents(n, tiles):
                for t in tiles:
                    if t == 0:
                        pe.wait_ge(qn_ready, TC * (n + 1))
                        pe.wait_ge(cn_ready, TC * (n + 1))
                        pe.wait_ge(rot_ready, n + 1)
                    if t >= 2:
                        pe.wait_ge(qkf_ready, TC * n + t - 1)
                    bank = banks[2 + t % 2]
                    nc.tensor.transpose(bank[:, 0:P], kn[:, t, 0:KVL + ROPE], ident[:])
                    nc.tensor.transpose(bank[:, P:2 * P], kn[:, t, KVL:], ident[:])
                    nc.tensor.transpose(bank[:, 2 * P:3 * P], qn[:, t, 0:P], ident[:])
                    nc.tensor.transpose(bank[:, 3 * P:4 * P], qn[:, t, P:2 * P], ident[:]).then_inc(kt_mm, 1)

            def chunk(n, more):
                pe.wait_ge(w_lo, NP_UP)
                for m in range(MT):
                    if m >= 2:
                        pe.wait_ge(hf_ready, MT * n + m - 1)
                    for half in range(2):
                        w = slice(half * FF + m * P, half * FF + (m + 1) * P)
                        mm = three(banks[4 + 2 * (m % 2) + half][:],
                                   [(w12h[:, k, w], w12l[:, k, w], xh[:, k, :], xl[:, k, :]) for k in range(KH)])
                    mm.then_inc(up_mm, 1)
                    turn_latents(n, TURN_AT.get(m, ()))
                if more:
                    turn_input(n + 1)
                pe.wait_ge(hl_ready, MT * (n + 1))
                pe.wait_ge(w_lo, NP)
                for t in range(TC):
                    cols = slice(t * P, (t + 1) * P)
                    three(banks[4 + t][:], [(hh[:, m, cols], hl[:, m, cols], w3h[:, m, :], w3l[:, m, :])
                                            for m in range(MT)]).then_inc(down_mm, 1)
                if more:
                    pe.wait_ge(qkf_ready, TC * (n + 1))
                    latents(n + 1, TC * (n + 1))

            pe.wait_ge(y_out, 16)
            turn_input(0)
            pe.wait_ge(w_lo, NP_LAT)
            latents(0, None)
            with pe.Fori(0, NCH - 1) as n:
                chunk(n, True)
            chunk(NCH - 1, False)


def attention(nc, io, scr, res):
    qk_hi, qk_lo, c16, wo_out = res["qk_hi"], res["qk_lo"], res["c16"], res["wo_out"]
    ROUNDS = B * PAIRS // 2
    RPB = PAIRS // 2
    BLK = 4
    HALF = S // 512
    CPH = ST // 2
    CPR = 4 * CPH
    WIN = CPR // 2
    GPC = 3
    SHORT, LONG = 0, 1
    with ExitStack() as ctx:
        sb = lambda n, s, d: ctx.enter_context(nc.sbuf_tensor(n + "_sb", s, d))
        sem = lambda n: ctx.enter_context(nc.semaphore(n))
        score = ctx.enter_context(nc.psum_tensor("score", [P, 4, 512], F32))
        flip = ctx.enter_context(nc.psum_tensor("flip", [P, 2, 512], F32))
        acc = ctx.enter_context(nc.psum_tensor("acc", [P, 512], F32))
        proj = ctx.enter_context(nc.psum_tensor("proj", [P, 512], F32))
        ident, mask = sb("ident2", [P, P], F32), sb("mask", [P, P], F32)
        ident_b, mask_b = sb("ident_b", [P, P], BF16), sb("mask_b", [P, P], BF16)
        cosT, sinT = sb("cosT", [P, 2, S], F32), sb("sinT", [P, S], F32)
        raw = [sb(f"wqk{j}", [P, 2, 2 * P + KVL], F32) for j in range(2)]
        wf = [sb(f"wq_f{j}", [P, 2, 2 * P], F32) for j in range(2)]
        wh = [sb(f"wq_h{j}", [P, 2, 2 * P], F32R) for j in range(2)]
        wl = [sb(f"wq_l{j}", [P, 2, 2 * P], F32R) for j in range(2)]
        qh, ql = sb("qh", [P, 4, S], F32R), sb("ql", [P, 4, S], F32R)
        rot = sb("rot", [P, 2, 512], F32)
        qf = sb("qf", [P, 2, 2, 512], F32)
        prob = [sb("prob_short", [P, 512], F32), sb("prob_long", [P, S], F32)]
        pth = [sb("pth_short", [P, 2, 512], F16), sb("pth_long", [P, 2, S], F16)]
        ptl = [sb("ptl_short", [P, 2, 512], F16), sb("ptl_long", [P, 2, S], F16)]
        shift, total = sb("shift", [P, CPR, 2], F32), sb("total", [P, 4, ST], F32)
        rtot = sb("rtot", [P, 4, ST], F32)
        o = sb("o", [P, 2, ST, P], F32)
        wv, wo, kvw2 = sb("wv", [P, 2, KVL], F32), sb("wo", [P, 2, H], F32), sb("kvw2", [P, 1], F32)
        wo_in, wo_mm, wo_ready = sem("wo_in"), sem("wo_mm"), sem("wo_ready")
        const_in, w_in = sem("const_in"), [sem("wq_in0"), sem("wq_in1")]
        proj_mm, proj_out, rot_add, qh_ready, ql_ready = (
            sem(n) for n in ("proj_mm", "proj_out", "rot_add", "qh_ready", "ql_ready"))
        score_mm, shift_ready, flip_mm, pth_ready, ptl_ready, pv_mm, rtot_ready, o_ready = (
            sem(n) for n in ("score_mm", "shift_ready", "flip_mm", "pth_ready", "ptl_ready", "pv_mm", "rtot_ready", "o_ready"))
        exp_ready = [sem("exp_short"), sem("exp_long")]
        o_out = [sem("o_out0"), sem("o_out1")]
        NCONST, cast_ready = 3, sem("cast_ready")
        absorb_mm, lat_ready, wh_ready, wl_ready = (sem(n) for n in ("absorb_mm", "wlat_ready", "wh_ready", "wl_ready"))
        first_mul, first_add, first_low = sem("first_mul"), sem("first_add"), sem("first_low")
        passed = sb("passed", [P, 3], F32)
        rot_in, rot_mul = [sem("rot_in0"), sem("rot_in1")], sem("rot_mul")
        window = lambda m: divmod(m + 1, WIN)
        PIECES = [(c, h) for c in range(HALF) for h in range(2)]
        PIECE_AT = [(0, "middle"), (0, "end"), (1, "middle"), (1, "end")]
        TAKE_AT = [(0, "middle"), (1, "start"), (1, "middle"), (2, "start")]
        HI_AT = [3, 3, 4, 5]
        ABSORB_AT, LAT_AT, WH_AT, WL_AT = 3, 4, 5, 6
        WO_AT, WO_TAKE_AT = 5, 6
        NPC = len(PIECES)
        o_dram = scr["o"].rearrange("(t p) c -> p t c", p=P)
        block = ctx.enter_context(nc.Block())

        def tile(m, kind):
            m %= CPR
            return m // CPH, ST - 1 - m % CPH if kind == LONG else m % CPH

        def banks_of(m, kind):
            return (1 + m % 2, 2) if kind == LONG else (0, 1)

        def score_of(m, kind):
            first, n = banks_of(m, kind)
            return score[:, first:first + n, :].rearrange("p b c -> p (b c)")[:, 0:(tile(m, kind)[1] + 1) * P]

        def turned(m, kind, c):
            i = tile(m, kind)[1]
            g = c if kind == LONG else 2
            return g, (GPC * m + g) % 2, slice(512 * c, 512 * c + min(BLK, i + 1 - BLK * c) * P)

        @block.sync
        def _(sp):
            def load_w(j, pair):
                sp.dma_start(raw[j][:].rearrange("p h c -> p (h c)"), io["wqk"][:, ds(pair, 1), :]).then_inc(w_in[j], 16)
                sp.dma_start(wf[j][:, :, KVL:KVL + 2 * ROPE], io["wqp"][:, ds(pair, 1), :, :]).then_inc(w_in[j], 16)

            def load_wo(pair):
                heads = slice(2 * pair, 2 * pair + 2) if isinstance(pair, int) else ds(pair * 2, 2)
                sp.dma_start(wv[:], io["wv"][:, heads, :]).then_inc(wo_in, 16)
                sp.dma_start(wo[:], io["wo"][:, heads, :]).then_inc(wo_in, 16)

            def swap_halves(c, taken):
                sp.wait_ge(proj_out, taken)
                half = ROPE // 2
                for h, base in ((0, KVL), (1, 0)):
                    for to, of in ((base, base + half), (base + half, base)):
                        sp.dma_start(rot[to:to + half, c, :], qf[of:of + half, c, h, :]).then_inc(rot_in[c], 16)

            load_w(0, 0)
            load_w(1, 1)
            for j, (dst, src) in enumerate(((ident, "ident"), (mask, "mask"))):
                sp.dma_start(dst[:], io[src]).then_inc(o_out[j], 16)
            for dst, src in ((sinT, "sinT"), (cosT, "cosT"), (kvw2, "kvw2")):
                sp.dma_start(dst[:], io[src]).then_inc(const_in, 16)
            load_wo(0)
            for c in range(HALF):
                swap_halves(c, 2 * c + 2)
            for j in range(2):
                sp.wait_ge(wl_ready, j + 1)
                load_w(j, 2 + j)
            with sp.Fori(0, ROUNDS) as it:
                b, pair = sp.snap(it // RPB), sp.snap((2 * it) % PAIRS)
                next_wo = sp.snap((it + 1) % PAIRS)
                ahead = [sp.snap((2 * it + 4) % PAIRS), sp.snap((2 * it + 5) % PAIRS)]
                for j in range(2):
                    for c in range(HALF):
                        swap_halves(c, NPC * (2 * it + 1 + j) + 2 * c + 2)
                    sp.wait_ge(wl_ready, 2 * it + j + 3)
                    load_w(j, ahead[j])
                    if j == 0:
                        sp.wait_ge(wo_mm, it + 1)
                        load_wo(next_wo)
                    sp.wait_ge(o_ready, 4 * (2 * it + j + 1) + 1)
                    sp.dma_start(o_dram[:, ds(b * ST, ST), ds((pair + j) * P, P)], o[:, j]).then_inc(o_out[j], 16)
            for j in range(2):
                sp.wait_ge(w_in[j], 32 * (ROUNDS + 2))
                sp.wait_ge(wo_in, 32 * (ROUNDS + 1))
                sp.wait_ge(o_out[j], 16 * (ROUNDS + 1))

        @block.tensor
        def _(pe):
            def absorb(j, loads):
                pe.wait_ge(w_in[j], loads)
                for t in range(2):
                    for h in range(2):
                        at = slice(t * P + h * KVL, t * P + (h + 1) * KVL)
                        mm = nc.tensor.matmul(proj[:, at], raw[j][:, h, t * P:(t + 1) * P], raw[j][:, h, 2 * P:],
                                              start=True, stop=True)
                mm.then_inc(absorb_mm, 1)

            def project(piece, b, j, out=proj[:]):
                c, h = PIECES[piece]
                cols = slice(h * P, (h + 1) * P)
                at = ds(b * S + c * 512, 512)
                terms = ((wh, 0, qk_hi, 2), (wh, 0, qk_lo, 2), (wl, 0, qk_hi, 2), (wh, 1, qk_hi, 3), (wl, 1, qk_hi, 3))
                for i, (w, t, q, kind) in enumerate(terms):
                    mm = nc.tensor.matmul(out, w[j][:, t, cols], q[:, kind, at], start=(i == 0), stop=(i == 4))
                mm.then_inc(proj_mm, 1)

            free_chunk, shared_chunk = lambda m: m % 2, lambda m: 1 - m % 2

            def scores(m, kind, b, c):
                head, i = tile(m, kind)
                keys = head % 2
                q = slice(i * P, (i + 1) * P)
                first, n = banks_of(m, kind)
                w = min(BLK, i + 1 - BLK * c) * P
                out = score[:, first + c, 0:w]
                at = ds(b * S + c * 512, w)
                nc.tensor.matmul(out, qh[:, head, q], qk_hi[:, keys, at], start=True, stop=False)
                nc.tensor.matmul(out, qh[:, head, q], qk_lo[:, keys, at], start=False, stop=False)
                last = c == n - 1
                mm = nc.tensor.matmul(out, ql[:, head, q], qk_hi[:, keys, at], start=False, stop=not last)
                if last:
                    mm = nc.tensor.matmul(out[:, w - P:w], ident_b[:], mask_b[:], start=False, stop=True)
                return mm

            def transposes(m, kind, before, c=0):
                g, bank, at = turned(m, kind, c)
                if before is not None:
                    pe.wait_ge(ptl_ready, before + g - 1)
                elif g == 2:
                    pe.wait_ge(ptl_ready, 1)
                for j in range(at.start // P, at.stop // P):
                    mm = nc.tensor.transpose(flip[:, bank, (j % BLK) * P:(j % BLK + 1) * P],
                                             prob[kind][:, j * P:(j + 1) * P], ident[:])
                mm.then_inc(flip_mm, 1)

            def values(m, kind, b):
                i = tile(m, kind)[1]
                slot = m % 2 if kind == SHORT else 3 - m % 2
                out = acc[:, slot * KVL:(slot + 1) * KVL]
                for j in range(i + 1):
                    p = slice(j * P, (j + 1) * P)
                    hi, lo = pth[kind][:, m % 2, p], ptl[kind][:, m % 2, p]
                    c = lambda half: c16[:, ds(b * ST + j, 1), half, :]
                    nc.tensor.matmul(out, hi, c(0), start=(j == 0), stop=False)
                    nc.tensor.matmul(out, hi, c(1), start=False, stop=False)
                    mm = nc.tensor.matmul(out, lo, c(0), start=False, stop=(j == i))
                return mm

            absorb(0, 32)
            pe.wait_ge(lat_ready, 1)
            absorb(1, 32)
            pe.wait_ge(wl_ready, 2)
            for piece in range(NPC):
                project(piece, 0, 0, score[:, piece, :])
            pe.wait_ge(cast_ready, 2)
            project(0, 0, 1)
            pe.wait_ge(proj_out, NPC + 1)
            project(1, 0, 1)
            pe.wait_ge(proj_out, NPC)
            pe.wait_ge(ql_ready, 4)
            scores(0, LONG, 0, 0)
            scores(0, LONG, 0, 1).then_inc(score_mm, 1)
            scores(0, SHORT, 0, 0).then_inc(score_mm, 1)
            scores(1, LONG, 0, free_chunk(1))
            pe.wait_ge(exp_ready[LONG], 1)
            scores(1, LONG, 0, shared_chunk(1)).then_inc(score_mm, 1)
            transposes(0, LONG, None, 0)
            transposes(0, LONG, None, 1)
            pe.wait_ge(exp_ready[SHORT], 1)
            scores(1, SHORT, 0, 0).then_inc(score_mm, 1)
            scores(2, LONG, 0, free_chunk(2))
            transposes(0, SHORT, None)
            with pe.Fori(0, ROUNDS) as it:
                b, b_next = it // RPB, ((it + 1) // RPB) % B

                def extra(m, where):
                    win, step = window(m)
                    if (step, where) in PIECE_AT:
                        piece = PIECE_AT.index((step, where))
                        if piece:
                            pe.wait_ge(proj_out, NPC * (2 * it + 1 + win) + piece)
                        else:
                            pe.wait_ge(wl_ready, 2 * it + win + 2)
                            if win == 1:
                                pe.wait_ge(wo_ready, it + 1)
                        project(piece, b if win == 0 else b_next, 1 - win % 2)
                    if step == ABSORB_AT and where == "end":
                        pe.wait_ge(proj_out, NPC * (2 * it + 2 + win))
                        absorb(win, 32 * (it + 2))
                    if (win, step) == (0, WO_AT):
                        h = 0 if where == "middle" else 1
                        if h == 0:
                            pe.wait_ge(lat_ready, 2 * it + 3)
                            pe.wait_ge(wo_in, 32 * (it + 1))
                        mm = nc.tensor.matmul(proj[h * KVL:(h + 1) * KVL, :], wv[:, h, :], wo[:, h, :], start=True, stop=True)
                        if h == 1:
                            mm.then_inc(wo_mm, 1)

                for m in range(CPR):
                    done, banks = CPR * it + m, GPC * (CPR * it + m)
                    b_ahead = b if m + 2 < CPR else b_next
                    pe.wait_ge(exp_ready[LONG], done + 2)
                    scores(m + 2, LONG, b_ahead, shared_chunk(m)).then_inc(score_mm, 1)
                    transposes(m + 1, LONG, banks + GPC, 0)
                    transposes(m + 1, LONG, banks + GPC, 1)
                    pe.wait_ge(exp_ready[SHORT], done + 2)
                    scores(m + 2, SHORT, b_ahead, 0).then_inc(score_mm, 1)
                    pe.wait_ge(ptl_ready, banks + 2)
                    if m % 2 == 0:
                        pe.wait_ge(o_ready, CPR // 2 * it + m // 2 + 1)
                    values(m, LONG, b)
                    pe.wait_ge(ptl_ready, banks + GPC)
                    values(m, SHORT, b).then_inc(pv_mm, 1)
                    extra(m, "middle")
                    if (m + 3) % WIN == 0:
                        pe.wait_ge(ql_ready, 8 * it + 4 + 4 * ((m + 3) // WIN))
                    scores(m + 3, LONG, b if m + 3 < CPR else b_next, free_chunk(m + 1))
                    transposes(m + 1, SHORT, banks + GPC)
                    extra(m, "end")

        def nth(it, win, i, per, ahead):
            return per * (2 * it + win) + ahead + i + 1

        @block.scalar
        def _(act):
            def exp(m, kind, scored):
                head, i = tile(m, kind)
                act.wait_ge(shift_ready, scored)
                m %= CPR
                nc.scalar.activation(prob[kind][:, 0:(i + 1) * P], score_of(m, kind), ACT.Exp,
                                     bias=shift[:, m, kind:kind + 1], scale=-1.0,
                                     accum_out=total[:, head, i:i + 1]).then_inc(exp_ready[kind], 1)

            def high(m, kind, before, c=0):
                g, bank, at = turned(m, kind, c)
                act.wait_ge(flip_mm, before + g + 1)
                nc.scalar.activation(pth[kind][:, m % 2, at], flip[:, bank, 0:at.stop - at.start],
                                     ACT.Copy).then_inc(pth_ready, 1)

            def query_high(j, k, c, h, rotated=rot_add):
                act.wait_ge(rotated, k)
                nc.scalar.activation(qh[:, 2 * j + h, c * 512:(c + 1) * 512], qf[:, c, h, :], ACT.Copy).then_inc(qh_ready, 1)

            def take(piece, k, out=proj[:]):
                c, h = PIECES[piece]
                act.wait_ge(proj_mm, k)
                nc.scalar.activation(qf[:, c, h, :], out, ACT.Copy).then_inc(proj_out, 1)

            def weights_latent(j, k):
                act.wait_ge(absorb_mm, k)
                for h, at in ((0, 0), (1, 2 * P - KVL)):
                    op = nc.scalar.activation(wf[j][:, :, at:at + KVL],
                                              proj[:, 0:2 * P].rearrange("p (t h c) -> p t h c", t=2, h=2)[:, :, h, :], ACT.Copy)
                op.then_inc(lat_ready, 1)

            def weights_high(j, k):
                act.wait_ge(lat_ready, k)
                nc.scalar.activation(wh[j][:], wf[j][:], ACT.Copy).then_inc(wh_ready, 1)

            for j in range(2):
                weights_latent(j, j + 1)
                weights_high(j, j + 1)
            for piece in range(NPC):
                take(piece, piece + 1, score[:, piece, :])
            for k in range(4):
                query_high(0, k + 1, k // 2, k % 2, first_add)
            act.wait_ge(ql_ready, 4)
            act.wait_ge(const_in, 16 * NCONST)
            take(0, NPC + 1)
            exp(0, LONG, 1)
            exp(0, SHORT, 2)
            high(0, LONG, 0, 0)
            high(0, LONG, 0, 1)
            exp(1, LONG, 3)
            high(0, SHORT, 0)
            with act.Fori(0, ROUNDS) as it:
                def extra(m, where):
                    win, step = window(m)
                    if (step, where) in TAKE_AT:
                        piece = TAKE_AT.index((step, where))
                        if piece == 0:
                            act.wait_ge(ql_ready, 4 * (2 * it + win + 1))
                        take(piece, nth(it, win, piece, NPC, NPC))
                    if (win, step, where) == (0, WO_TAKE_AT, "middle"):
                        act.wait_ge(wo_mm, it + 1)
                        nc.scalar.activation(wo_out[:].bitcast(F32)[:, ds(it, 1), :], proj[:].rearrange("p (a c) -> p a c", a=1),
                                             ACT.Copy, scale=kvw2[:, 0:1]).then_inc(wo_ready, 1)
                    if where == "middle":
                        for i in range(4):
                            if HI_AT[i] == step:
                                query_high(1 - win, nth(it, win, i, 4, 4), i // 2, i % 2)
                    if where == "end":
                        if step == LAT_AT:
                            weights_latent(win, nth(it, win, 0, 1, 2))
                        if step == WH_AT:
                            weights_high(win, nth(it, win, 0, 1, 2))

                for m in range(CPR):
                    done, banks = CPR * it + m, GPC * (CPR * it + m)
                    extra(m, "start")
                    exp(m + 1, SHORT, 2 * done + 4)
                    high(m + 1, LONG, banks + GPC, 0)
                    high(m + 1, LONG, banks + GPC, 1)
                    exp(m + 2, LONG, 2 * done + 5)
                    extra(m, "middle")
                    high(m + 1, SHORT, banks + GPC)
                    extra(m, "end")

        @block.gpsimd
        def _(pool):
            def query_low(j, c, h, k):
                pool.wait_ge(qh_ready, k)
                at = slice(c * 512, (c + 1) * 512)
                nc.gpsimd.tensor_tensor(ql[:, 2 * j + h, at], qf[:, c, h, :], qh[:, 2 * j + h, at].bitcast(F32),
                                        ALU.subtract).then_inc(ql_ready, 1)

            def pair(j, before):
                for c in range(HALF):
                    at = slice(c * 512, (c + 1) * 512)
                    if c == 1:
                        pool.wait_ge(rot_add, 4 * before + 2)
                    pool.wait_ge(rot_in[c], 64 * (before + 1))
                    nc.gpsimd.tensor_tensor(rot[:, c, :], rot[:, c, :], sinT[:, at], ALU.mult)
                    for h in range(2):
                        op = nc.gpsimd.tensor_tensor(qf[:, c, h, :], qf[:, c, h, :], cosT[:, h, at], ALU.mult)
                    op.then_inc(rot_mul, 1)
                    pool.wait_ge(rot_mul, 2 * before + c + 1)
                    for h, rows in ((0, slice(KVL, P)), (1, slice(0, ROPE))):
                        if h == 1:
                            pool.wait_ge(rot_add, 4 * before + 2 * c + 1)
                        nc.gpsimd.tensor_tensor(qf[rows, c, h, :], qf[rows, c, h, :], rot[rows, c, :],
                                                ALU.add).then_inc(rot_add, 1)
                for c in range(HALF):
                    for h in range(2):
                        query_low(j, c, h, 4 * before + 2 * c + h + 1)

            pool.wait_ge(const_in, 16 * NCONST)
            pool.wait_ge(first_low, 4)
            for i, (semaphore, per_pair) in enumerate(((rot_mul, 2), (rot_add, 4), (ql_ready, 4))):
                nc.gpsimd.memset(passed[:, i:i + 1], 0.0).then_inc(semaphore, per_pair)
            with pool.Fori(0, ROUNDS) as it:
                pair(1, 2 * it + 1)
                pair(0, 2 * it + 2)

        @block.vector
        def _(dve):
            def least(m, kind, scored):
                dve.wait_ge(score_mm, scored)
                m %= CPR
                nc.vector.tensor_reduce(shift[:, m, kind:kind + 1], score_of(m, kind), AX.X, ALU.min).then_inc(shift_ready, 1)

            def low(m, kind, before, c=0):
                g, bank, at = turned(m, kind, c)
                dve.wait_ge(pth_ready, before + g + 1)
                nc.vector.tensor_tensor(ptl[kind][:, m % 2, at], flip[:, bank, 0:at.stop - at.start],
                                        pth[kind][:, m % 2, at], ALU.subtract).then_inc(ptl_ready, 1)

            def weights_low(j, k):
                dve.wait_ge(wh_ready, k)
                nc.vector.tensor_tensor(wl[j][:], wf[j][:], wh[j][:].bitcast(F32), ALU.subtract).then_inc(wl_ready, 1)

            def of_two(a, m):
                return a.rearrange("p (a b) -> p a b", b=2)[:, slice(0, 4, 3) if m % CPH < 2 else slice(1, 3), :]

            def inverse_sums(m):
                head = m // CPH
                nc.vector.reciprocal(of_two(rtot[:, head], m), of_two(total[:, head], m)).then_inc(rtot_ready, 1)

            def outputs(m, done, it):
                head, h = m // CPH, m // CPH % 2
                dve.wait_ge(pv_mm, done)
                dve.wait_ge(rtot_ready, CPR // 2 * it + m // 2 + 1)
                if m % WIN == 1:
                    dve.wait_ge(o_out[head // 2], 16 * (it + 1))
                two = slice(0, 4, 3) if m % CPH < 2 else slice(1, 3)
                nc.vector.tensor_tensor(
                    o[:, head // 2, :, h * KVL:(h + 1) * KVL].rearrange("p (a b) c -> p a b c", b=2)[:, two],
                    acc[:, 0:BLK * KVL].rearrange("p (a b c) -> p a b c", a=2, b=2),
                    of_two(rtot[:, head], m).unsqueeze(3).broadcast_to([P, 2, 2, KVL]), ALU.mult).then_inc(o_ready, 1)

            nc.vector.memset(rtot[:], 0.0).then_inc(o_ready, 1)
            for j, (to, of) in enumerate(((ident_b, ident), (mask_b, mask))):
                dve.wait_ge(o_out[j], 16)
                nc.vector.tensor_copy(to[:], of[:]).then_inc(cast_ready, 1)
            for j in range(2):
                weights_low(j, j + 1)
            dve.wait_ge(const_in, 16 * NCONST)
            for c in range(HALF):
                at = slice(c * 512, (c + 1) * 512)
                dve.wait_ge(rot_in[c], 64)
                nc.vector.tensor_tensor(rot[:, c, :], rot[:, c, :], sinT[:, at], ALU.mult)
                for h in range(2):
                    op = nc.vector.tensor_tensor(qf[:, c, h, :], qf[:, c, h, :], cosT[:, h, at], ALU.mult)
                op.then_inc(first_mul, 1)
                dve.wait_ge(first_mul, c + 1)
                for h, rows in ((0, slice(KVL, P)), (1, slice(0, ROPE))):
                    nc.vector.tensor_tensor(qf[rows, c, h, :], qf[rows, c, h, :], rot[rows, c, :],
                                            ALU.add).then_inc(first_add, 1)
            for c in range(HALF):
                at = slice(c * 512, (c + 1) * 512)
                for h in range(2):
                    dve.wait_ge(qh_ready, 2 * c + h + 1)
                    nc.vector.tensor_tensor(ql[:, h, at], qf[:, c, h, :], qh[:, h, at].bitcast(F32),
                                            ALU.subtract).then_inc(first_low, 1)
            least(0, LONG, 1)
            least(0, SHORT, 2)
            least(1, LONG, 3)
            low(0, LONG, 0, 0)
            low(0, LONG, 0, 1)
            least(1, SHORT, 4)
            low(0, SHORT, 0)
            with dve.Fori(0, ROUNDS) as it:
                for m in range(CPR):
                    done, banks = CPR * it + m, GPC * (CPR * it + m)
                    win, step = window(m)
                    if m % 2 == 1:
                        inverse_sums(m)
                    least(m + 2, LONG, 2 * done + 5)
                    low(m + 1, LONG, banks + GPC, 0)
                    low(m + 1, LONG, banks + GPC, 1)
                    least(m + 2, SHORT, 2 * done + 6)
                    low(m + 1, SHORT, banks + GPC)
                    if m % 2 == 1:
                        outputs(m, done + 1, it)
                    if step == WL_AT:
                        weights_low(win, nth(it, win, 0, 1, 2))


def combine(nc, io, scr, wol):
    NR = NT // 2
    with ExitStack() as ctx:
        sb = lambda n, s, d: ctx.enter_context(nc.sbuf_tensor(n + "_sb", s, d))
        sem = lambda n: ctx.enter_context(nc.semaphore(n))
        flip = [ctx.enter_context(nc.psum_tensor(f"turn{i}", [P, 512], F32)) for i in range(4)]
        acc = [ctx.enter_context(nc.psum_tensor(f"sum{i}", [P, 512], F32)) for i in range(2)]
        ident = sb("ident3", [P, P], F32)
        woh = sb("woh", [P, PAIRS, H], F32R)
        o = sb("o_nat", [P, 2, PAIRS * P], F32)
        oh, ol = sb("oT_hi", [P, 2, PAIRS, P], F32R), sb("oT_lo", [P, 2, PAIRS, P], F32R)
        y = sb("y_in", [P, 2, H], F32)
        woh_ready, wol_ready = sem("woh_ready"), sem("wol_ready")
        in_w, in_t, in_y = sem("ident_in"), [sem("tile_in0"), sem("tile_in1")], [sem("y_in0"), sem("y_in1")]
        turn_mm, oh_ready, ol_ready, sum_mm, y_ready, stored = (
            sem(n) for n in ("turn_mm", "oh_ready", "ol_ready", "sum_mm", "sum_ready", "out_stored"))
        G = PAIRS // 4
        block = ctx.enter_context(nc.Block())

        @block.sync
        def _(sp):
            def load(t, j):
                sp.dma_start(o[:, j, :], scr["o"].rearrange("(t p) c -> p t c", p=P)[:, ds(t, 1), :]).then_inc(in_t[j], 16)

            sp.dma_start(ident[:], io["ident"]).then_inc(in_w, 16)
            load(0, 0)
            load(1, 1)
            with sp.Fori(0, NR) as it:
                after = [sp.snap((2 * it + j + 2) % NT) for j in range(2)]
                for j in range(2):
                    sp.wait_ge(turn_mm, G * (2 * it + j + 1))
                    load(after[j], j)
            for j in range(2):
                sp.wait_ge(in_t[j], 16 * (NR + 1))

        @block.gpsimd
        def _(pool):
            def load(t, j):
                pool.dma_start(y[:, j, :], scr["y"][:, ds(t, 1), :]).then_inc(in_y[j], 16)

            load(0, 0)
            load(1, 1)
            with pool.Fori(0, NR) as it:
                after = [pool.snap((2 * it + j + 2) % NT) for j in range(2)]
                for j in range(2):
                    pool.wait_ge(y_ready, 2 * it + j + 1)
                    pool.dma_start(io["out"][:, ds(2 * it + j, 1), :], y[:, j:j + 1, :]).then_inc(stored, 16)
                    pool.wait_ge(stored, 16 * (2 * it + j + 1))
                    load(after[j], j)
            for j in range(2):
                pool.wait_ge(in_y[j], 16 * (NR + 1))

        @block.tensor
        def _(pe):
            def turn(j, tile, loads):
                pe.wait_ge(in_t[j], loads)
                for g in range(G):
                    if tile is not None:
                        pe.wait_ge(ol_ready, G * tile + g - G + 1)
                    for k in range(4):
                        pair = 4 * g + k
                        mm = nc.tensor.transpose(flip[g][:, k * P:(k + 1) * P], o[:, j, pair * P:(pair + 1) * P], ident[:])
                    mm.then_inc(turn_mm, 1)

            pe.wait_ge(in_w, 16)
            turn(0, None, 16)
            with pe.Fori(0, NR) as it:
                for j in range(2):
                    n = 2 * it + j
                    turn(1 - j, n + 1, 16 * (it + 1 + j))
                    pe.wait_ge(ol_ready, G * (n + 1))
                    for pair in range(PAIRS):
                        pe.wait_ge(wol_ready, pair + 1)
                        nc.tensor.matmul(acc[j][:], oh[:, j, pair, :], woh[:, pair, :], start=(pair == 0), stop=False)
                        nc.tensor.matmul(acc[j][:], oh[:, j, pair, :], wol[:, pair, :], start=False, stop=False)
                        mm = nc.tensor.matmul(acc[j][:], ol[:, j, pair, :], woh[:, pair, :], start=False,
                                              stop=(pair == PAIRS - 1))
                    mm.then_inc(sum_mm, 1)

        @block.scalar
        def _(act):
            def high(j, first):
                for g in range(G):
                    act.wait_ge(turn_mm, first + g + 1)
                    nc.scalar.activation(oh[:, j, 4 * g:4 * g + 4, :], flip[g][:].rearrange("p (k c) -> p k c", k=4),
                                         ACT.Copy).then_inc(oh_ready, 1)
            high(0, 0)
            for p in range(PAIRS):
                nc.scalar.activation(woh[:, p, :], wol[:, p, :].bitcast(F32), ACT.Copy).then_inc(woh_ready, 1)
            with act.Fori(0, NR) as it:
                for j in range(2):
                    high(1 - j, G * (2 * it + j + 1))

        @block.vector
        def _(dve):
            def low(j, first):
                for g in range(G):
                    dve.wait_ge(oh_ready, first + g + 1)
                    at = slice(4 * g, 4 * g + 4)
                    nc.vector.tensor_tensor(ol[:, j, at, :], flip[g][:].rearrange("p (k c) -> p k c", k=4),
                                            oh[:, j, at, :].bitcast(F32), ALU.subtract).then_inc(ol_ready, 1)
            low(0, 0)
            for p in range(PAIRS):
                dve.wait_ge(woh_ready, p + 1)
                nc.vector.tensor_tensor(wol[:, p, :], wol[:, p, :].bitcast(F32), woh[:, p, :].bitcast(F32),
                                        ALU.subtract).then_inc(wol_ready, 1)
            with dve.Fori(0, NR) as it:
                for j in range(2):
                    low(1 - j, G * (2 * it + j + 1))
                    dve.wait_ge(sum_mm, 2 * it + j + 1)
                    dve.wait_ge(in_y[j], 16 * (it + 1))
                    nc.vector.tensor_tensor(y[:, j, :], acc[j][:], y[:, j, :], ALU.add).then_inc(y_ready, 1)


def build(nc, io):
    scr = {n: nc.dram_tensor(n, s, F32, kind="Internal").ap() for n, s in (
        ("y", (P, NT, H)), ("o", (TOK, PAIRS * P)))}
    with ExitStack() as ctx:
        res = {n: ctx.enter_context(nc.sbuf_tensor(n, s, d)) for n, s, d in (
            ("qk_hi", [P, 4, TOK], F32R), ("qk_lo", [P, 3, TOK], F32R), ("c16", [P, NT, 2, KVL], F16))}
        dense(nc, io, scr, res)
        res["wo_out"] = ctx.enter_context(nc.sbuf_tensor("wo_out", [P, PAIRS, H], F32R))
        attention(nc, io, scr, res)
        combine(nc, io, scr, res["wo_out"])


def _tables():
    half = ROPE // 2
    expo = (np.arange(0, ROPE, 2, dtype=np.float32) / np.float32(ROPE)).astype(np.float64)
    freqs = np.float32(1.0) / (10000.0 ** expo).astype(np.float32)
    ang = np.outer(np.arange(S, dtype=np.float32), freqs).astype(np.float32)
    cos, sin = np.cos(ang).astype(np.float32), np.sin(ang).astype(np.float32)
    one = np.ones((KVL, S), np.float32)
    cosT = np.concatenate([cos.T, cos.T])
    rot = np.concatenate([-sin.T, sin.T])
    tok = lambda a: np.ascontiguousarray(a.reshape(ST, P, half).transpose(1, 0, 2))
    future = np.arange(P)[None, :] > np.arange(P)[:, None]
    return {
        "cos_tok": tok(cos), "sin_tok": tok(sin),
        "cosT": np.stack([np.concatenate([one, cosT]), np.concatenate([cosT, one])], 1),
        "sinT": np.concatenate([rot, rot]),
        "ident": np.eye(P, dtype=np.float32),
        "mask": np.where(future, 3.0e38, 0.0).astype(np.float32),
    }


def _layout(x):
    a = {k: np.asarray(v) for k, v in x.items()}
    half = ROPE // 2
    eo = np.concatenate([np.arange(0, ROPE, 2), np.arange(1, ROPE, 2)])
    wqb = a["L0_attn_wq_b"].reshape(NH, NOPE + ROPE, QL)
    pe = wqb[:, NOPE:, :]
    rows = np.concatenate([np.arange(QL), np.arange(P, QL)])
    wqp = pe[:, eo][:, :, rows].reshape(PAIRS, 2, ROPE, 2, P)
    wqp = wqp.transpose(4, 0, 3, 1, 2).reshape(P, PAIRS, 2, 2 * ROPE)
    wqn = wqb[:, :NOPE][:, :, rows].transpose(1, 0, 2)
    wkva = a["L0_attn_wkv_a"]
    lat = np.concatenate([a["L0_attn_wq_a"], wkva[:KVL], wkva[KVL:][eo]], 0)
    wkvb = a["L0_attn_wkv_b"].reshape(NH, NOPE + VD, KVL)
    kt = lambda w: w.T.reshape(w.shape[1] // P, P, w.shape[0]).transpose(1, 0, 2)
    qnw, kvw = a["L0_attn_q_norm_w"], a["L0_attn_kv_norm_w"]
    col = lambda v: v.reshape(-1, P).T
    out = {
        "x": a["L0_attn_x"].reshape(NT, P, H).transpose(1, 0, 2),
        "wqp": wqp,
        "wqk": np.concatenate([wqn, wkvb[:, :NOPE].transpose(1, 0, 2)], 2).reshape(P, PAIRS, 2 * (2 * P + KVL)),
        "wv": wkvb[:, NOPE:].transpose(1, 0, 2),
        "wo": a["L0_attn_wo"].T.reshape(NH, VD, H).transpose(1, 0, 2),
        "w_lat": kt(lat), "w12": kt(a["L0_ffn_w12"]), "w3": kt(a["L0_ffn_w3"]),
        "b12": col(a["L0_ffn_b12"]), "b3": a["L0_ffn_b3"].reshape(1, H),
        "qnw0": qnw[:P].reshape(P, 1), "qnw1": np.concatenate([qnw[P:], qnw[P:]]).reshape(P, 1),
        "kvw": kvw.reshape(KVL, 1), "kvw2": np.concatenate([kvw, kvw]).reshape(P, 1),
        **_tables(),
    }
    return {k: np.ascontiguousarray(v) for k, v in out.items()}


def kernel(**inputs):
    import concourse.bacc as _bacc
    from concourse.bass_utils import run_bass_kernel_spmd as _run

    nc = _bacc.Bacc("TRN2", target_bir_lowering=False, num_devices=1)
    arrays = _layout(inputs)
    io = {k: nc.dram_tensor(k, v.shape, mybir.dt.from_np(v.dtype), kind="ExternalInput").ap()
          for k, v in arrays.items()}
    io["out"] = nc.dram_tensor("out", (P, NT, H), F32, kind="ExternalOutput").ap()
    build(nc, io)
    r = _run(nc, [arrays], core_ids=[0])
    return r.results[0]["out"].transpose(1, 0, 2).reshape(B, S, H)
```
